# Optimizing a Trainium2 kernel written in Bass

```python
import numpy as np
import jax
import jax.numpy as jnp

def _softmax(x, axis=-1):
    return jax.nn.softmax(x, axis=axis)

def _gelu(x):
    return jax.nn.gelu(x, approximate=True)

def _silu(x):
    return jax.nn.silu(x)

def _sigmoid(x):
    return jax.nn.sigmoid(x)

def _layernorm(x, axis=-1, eps=1e-05):
    m = jnp.mean(x, axis=axis, keepdims=True)
    v = jnp.var(x, axis=axis, keepdims=True)
    return (x - m) / jnp.sqrt(v + eps)

def _scatter_add(tgt, idx, src, axis=0):
    return tgt.at[idx].add(src)

def _segment_sum(src, seg, n):
    return jax.ops.segment_sum(src, seg, n)
kernel_name = 'mk_adj_resnorm_d1_adj_r2_eda5fe'

def setup_inputs(seed: int=0):
    np.random.seed(seed)
    _w = jnp.asarray

    def _rec_inputs():
        import jax
        import jax.numpy as jnp
        _gk = jax.random.key(seed)
        x = 1.444e-06 + 0.02 * jax.random.normal(jax.random.fold_in(_gk, 1), (64, 128, 512), jnp.float32)
        _w = (1.0 + jnp.arange(128, dtype=jnp.float32)) ** (-0.5)
        _w = _w / _w.mean()
        _pij = jnp.clip(0.125 * _w[:, None] * _w[None, :], 0.0, 1.0)
        _a = jax.random.uniform(jax.random.fold_in(_gk, 2), (64, 128, 128)) < _pij
        _a = jnp.logical_or(_a, jnp.eye(128, dtype=bool))
        _af = _a.astype(jnp.float32)
        adj = _af
        return (x, adj)
    x, adj = _rec_inputs()

    def _L0_gnn_setup():
        import jax, jax.numpy as jnp
        import numpy as np
        B, N, D, H = (4, 1024, 512, 8)
        HD = D // H
        SCALE = HD ** (-0.5)
        LN_EPS = 1e-05

        def _lin(x, w, b):
            return x @ w.T + b

        def _ln(x, g, b):
            m = x.mean(-1, keepdims=True)
            v = ((x - m) ** 2).mean(-1, keepdims=True)
            return (x - m) / jnp.sqrt(v + LN_EPS) * g + b

        def _attn(q, k, v, mask):
            Bq, Nt, _ = q.shape
            Ns = k.shape[1]
            qh = q.reshape(Bq, Nt, H, HD).transpose(0, 2, 1, 3)
            kh = k.reshape(Bq, Ns, H, HD).transpose(0, 2, 1, 3)
            vh = v.reshape(Bq, Ns, H, HD).transpose(0, 2, 1, 3)
            scores = jnp.einsum('bhid,bhjd->bhij', qh, kh) * SCALE
            scores = jnp.where(mask[:, None] > 0, scores, -jnp.inf)
            w = jax.nn.softmax(scores, axis=-1)
            out = jnp.einsum('bhij,bhjd->bhid', w, vh)
            return out.transpose(0, 2, 1, 3).reshape(Bq, Nt, D)
        key = jax.random.key(seed)
        ks = jax.random.split(key, 16)
        pe = jax.random.normal(ks[0], (B, N, D), jnp.float32) * 0.02
        inc = jax.random.randint(ks[1], (B, N, N), 0, 2).astype(jnp.float32)
        inc = jnp.maximum(inc, jnp.eye(N, dtype=jnp.float32)[None])

        def w(k, o, i):
            return jax.random.normal(k, (o, i), jnp.float32) / np.sqrt(i)
        inp = {'prompt_embeddings': pe, 'incidence_matrix': inc, 'n2e_q_w': w(ks[2], D, D), 'n2e_q_b': jnp.zeros((D,), jnp.float32), 'n2e_k_w': w(ks[3], D, D), 'n2e_k_b': jnp.zeros((D,), jnp.float32), 'n2e_v_w': w(ks[4], D, D), 'n2e_v_b': jnp.zeros((D,), jnp.float32), 'e2n_q_w': w(ks[5], D, D), 'e2n_q_b': jnp.zeros((D,), jnp.float32), 'e2n_k_w': w(ks[6], D, D), 'e2n_k_b': jnp.zeros((D,), jnp.float32), 'e2n_v_w': w(ks[7], D, D), 'e2n_v_b': jnp.zeros((D,), jnp.float32), 'norm1_g': jnp.ones((D,), jnp.float32), 'norm1_b': jnp.zeros((D,), jnp.float32), 'norm2_g': jnp.ones((D,), jnp.float32), 'norm2_b': jnp.zeros((D,), jnp.float32), 'norm3_g': jnp.ones((D,), jnp.float32), 'norm3_b': jnp.zeros((D,), jnp.float32), 'ffn_w1': w(ks[8], 4 * D, D), 'ffn_b1': jnp.zeros((4 * D,), jnp.float32), 'ffn_w2': w(ks[9], D, 4 * D), 'ffn_b2': jnp.zeros((D,), jnp.float32)}
        return inp
    _L0_gnn_all = _L0_gnn_setup()
    _L0_gnn_in = {k: v for k, v in _L0_gnn_all.items() if k in ('n2e_q_w', 'n2e_q_b', 'n2e_k_w', 'n2e_k_b', 'n2e_v_w', 'n2e_v_b', 'e2n_q_w', 'e2n_q_b', 'e2n_k_w', 'e2n_k_b', 'e2n_v_w', 'e2n_v_b', 'norm1_g', 'norm1_b', 'norm2_g', 'norm2_b', 'norm3_g', 'norm3_b', 'ffn_w1', 'ffn_b1', 'ffn_w2', 'ffn_b2')}
    del _L0_gnn_all
    return {'x': x, 'adj': adj, 'L0_gnn_n2e_q_w': _L0_gnn_in['n2e_q_w'], 'L0_gnn_n2e_q_b': _L0_gnn_in['n2e_q_b'], 'L0_gnn_n2e_k_w': _L0_gnn_in['n2e_k_w'], 'L0_gnn_n2e_k_b': _L0_gnn_in['n2e_k_b'], 'L0_gnn_n2e_v_w': _L0_gnn_in['n2e_v_w'], 'L0_gnn_n2e_v_b': _L0_gnn_in['n2e_v_b'], 'L0_gnn_e2n_q_w': _L0_gnn_in['e2n_q_w'], 'L0_gnn_e2n_q_b': _L0_gnn_in['e2n_q_b'], 'L0_gnn_e2n_k_w': _L0_gnn_in['e2n_k_w'], 'L0_gnn_e2n_k_b': _L0_gnn_in['e2n_k_b'], 'L0_gnn_e2n_v_w': _L0_gnn_in['e2n_v_w'], 'L0_gnn_e2n_v_b': _L0_gnn_in['e2n_v_b'], 'L0_gnn_norm1_g': _L0_gnn_in['norm1_g'], 'L0_gnn_norm1_b': _L0_gnn_in['norm1_b'], 'L0_gnn_norm2_g': _L0_gnn_in['norm2_g'], 'L0_gnn_norm2_b': _L0_gnn_in['norm2_b'], 'L0_gnn_norm3_g': _L0_gnn_in['norm3_g'], 'L0_gnn_norm3_b': _L0_gnn_in['norm3_b'], 'L0_gnn_ffn_w1': _L0_gnn_in['ffn_w1'], 'L0_gnn_ffn_b1': _L0_gnn_in['ffn_b1'], 'L0_gnn_ffn_w2': _L0_gnn_in['ffn_w2'], 'L0_gnn_ffn_b2': _L0_gnn_in['ffn_b2']}

def reference(x, adj, L0_gnn_n2e_q_w, L0_gnn_n2e_q_b, L0_gnn_n2e_k_w, L0_gnn_n2e_k_b, L0_gnn_n2e_v_w, L0_gnn_n2e_v_b, L0_gnn_e2n_q_w, L0_gnn_e2n_q_b, L0_gnn_e2n_k_w, L0_gnn_e2n_k_b, L0_gnn_e2n_v_w, L0_gnn_e2n_v_b, L0_gnn_norm1_g, L0_gnn_norm1_b, L0_gnn_norm2_g, L0_gnn_norm2_b, L0_gnn_norm3_g, L0_gnn_norm3_b, L0_gnn_ffn_w1, L0_gnn_ffn_b1, L0_gnn_ffn_w2, L0_gnn_ffn_b2):
    import jax
    import jax.numpy as jnp

    def _L0_gnn_ref(prompt_embeddings, incidence_matrix, n2e_q_w, n2e_q_b, n2e_k_w, n2e_k_b, n2e_v_w, n2e_v_b, e2n_q_w, e2n_q_b, e2n_k_w, e2n_k_b, e2n_v_w, e2n_v_b, norm1_g, norm1_b, norm2_g, norm2_b, norm3_g, norm3_b, ffn_w1, ffn_b1, ffn_w2, ffn_b2):
        import jax, jax.numpy as jnp
        import numpy as np
        B, N, D, H = (4, 1024, 512, 8)
        HD = D // H
        SCALE = HD ** (-0.5)
        LN_EPS = 1e-05

        def _lin(x, w, b):
            return x @ w.T + b

        def _ln(x, g, b):
            m = x.mean(-1, keepdims=True)
            v = ((x - m) ** 2).mean(-1, keepdims=True)
            return (x - m) / jnp.sqrt(v + LN_EPS) * g + b

        def _attn(q, k, v, mask):
            Bq, Nt, _ = q.shape
            Ns = k.shape[1]
            qh = q.reshape(Bq, Nt, H, HD).transpose(0, 2, 1, 3)
            kh = k.reshape(Bq, Ns, H, HD).transpose(0, 2, 1, 3)
            vh = v.reshape(Bq, Ns, H, HD).transpose(0, 2, 1, 3)
            scores = jnp.einsum('bhid,bhjd->bhij', qh, kh) * SCALE
            scores = jnp.where(mask[:, None] > 0, scores, -jnp.inf)
            w = jax.nn.softmax(scores, axis=-1)
            out = jnp.einsum('bhij,bhjd->bhid', w, vh)
            return out.transpose(0, 2, 1, 3).reshape(Bq, Nt, D)
        pe = prompt_embeddings
        n2e_mask = incidence_matrix.transpose(0, 2, 1)
        eq = _lin(pe, n2e_q_w, n2e_q_b)
        nk = _lin(pe, n2e_k_w, n2e_k_b)
        nv = _lin(pe, n2e_v_w, n2e_v_b)
        edge_features = _attn(eq, nk, nv, n2e_mask)
        edge_features = _ln(edge_features + pe, norm1_g, norm1_b)
        nq = _lin(pe, e2n_q_w, e2n_q_b)
        ek = _lin(edge_features, e2n_k_w, e2n_k_b)
        ev = _lin(edge_features, e2n_v_w, e2n_v_b)
        node_updates = _attn(nq, ek, ev, incidence_matrix)
        node_features = _ln(pe + node_updates, norm2_g, norm2_b)
        h = jax.nn.gelu(_lin(node_features, ffn_w1, ffn_b1), approximate=False)
        out = _ln(node_features + _lin(h, ffn_w2, ffn_b2), norm3_g, norm3_b)
        return out
    x = _layernorm(x + _L0_gnn_ref(x, adj, L0_gnn_n2e_q_w, L0_gnn_n2e_q_b, L0_gnn_n2e_k_w, L0_gnn_n2e_k_b, L0_gnn_n2e_v_w, L0_gnn_n2e_v_b, L0_gnn_e2n_q_w, L0_gnn_e2n_q_b, L0_gnn_e2n_k_w, L0_gnn_e2n_k_b, L0_gnn_e2n_v_w, L0_gnn_e2n_v_b, L0_gnn_norm1_g, L0_gnn_norm1_b, L0_gnn_norm2_g, L0_gnn_norm2_b, L0_gnn_norm3_g, L0_gnn_norm3_b, L0_gnn_ffn_w1, L0_gnn_ffn_b1, L0_gnn_ffn_w2, L0_gnn_ffn_b2), axis=-1)
    return x

_drawn_inputs = setup_inputs


def setup_inputs(seed=0):
    import zlib

    import numpy as np

    out = dict(_drawn_inputs(seed))
    spreads = {'L0_gnn_n2e_q_b': (0.0, 2.0),
     'L0_gnn_n2e_k_b': (0.0, 2.0),
     'L0_gnn_n2e_v_b': (0.0, 0.1),
     'L0_gnn_e2n_q_b': (0.0, 0.8),
     'L0_gnn_e2n_k_b': (0.0, 2.0),
     'L0_gnn_e2n_v_b': (0.0, 0.1),
     'L0_gnn_norm1_g': (1.0, 0.2),
     'L0_gnn_norm1_b': (0.0, 0.1),
     'L0_gnn_norm2_g': (1.0, 0.2),
     'L0_gnn_norm2_b': (0.0, 0.1),
     'L0_gnn_norm3_g': (1.0, 0.2),
     'L0_gnn_norm3_b': (0.0, 0.1),
     'L0_gnn_ffn_b1': (0.0, 0.1),
     'L0_gnn_ffn_b2': (0.0, 0.1)}
    factors = {'L0_gnn_n2e_q_w': 64.0,
     'L0_gnn_n2e_k_w': 64.0,
     'L0_gnn_e2n_q_w': 26.286,
     'L0_gnn_e2n_k_w': 8.0}
    for name, (base, spread) in spreads.items():
        noise = np.random.default_rng([zlib.crc32(name.encode()), seed]).standard_normal(out[name].shape)
        drawn = base * np.exp(spread * noise) if base else spread * noise
        out[name] = jnp.asarray(drawn.astype(out[name].dtype))
    for name, factor in factors.items():
        out[name] = (out[name] * factor).astype(out[name].dtype)
    return out
```

```python
from contextlib import ExitStack

import concourse.bass as bass
from concourse import mybir

P = 128
D = 512
C = D // P
B = 64
T = B * P
GB = 4
GT = GB * P
NG = B // GB
H = 8
HD = D // H
FF = 4 * D
FC = FF // P
SCALE = float(HD) ** -0.5
EPS = 1e-5
MASKED = -1e30
LARGEST = 3e38

F32 = mybir.dt.float32
F32R = mybir.dt.float32r
F16 = mybir.dt.float16
BF16 = mybir.dt.bfloat16
ALU = mybir.AluOpType
ACT = mybir.ActivationFunctionType

PROJ = GB + 2 * C
UNIT = GB * 2


def wait(engine, semaphore, value):
    if isinstance(value, int) and value <= 0:
        return
    engine.wait_ge(semaphore, value)


def gate(engine, semaphore, value, scratch):
    if not isinstance(value, int):
        engine.wait_ge(semaphore, value)
        engine.memset(scratch, 0.0)
    else:
        engine.wait_ge(semaphore, value)


def pool_gate(engine, semaphore, value, scratch):
    engine.wait_ge(semaphore, value)
    if not isinstance(value, int):
        engine.tensor_tensor(scratch[:, 0:1], scratch[:, 1:2], scratch[:, 2:3], ALU.add)


def over_groups(engine, body):
    body(0, 0)
    body(1, 1)
    with engine.Fori(1, NG // 2 - 1) as i:
        body(2 * i, 0)
        body(2 * i + 1, 1)
    body(NG - 2, 0)
    body(NG - 1, 1)
    body(NG, 0)


def starts(group):
    return isinstance(group, int) and group == 0


def ends(group):
    return isinstance(group, int) and group == NG


def whole(group):
    return not (isinstance(group, int) and group >= NG - 1)


def row(vector):
    return vector.rearrange("(a d) -> a d", a=1).to_broadcast([P, D])


def attention_pass(nc, name, query_source, value_source, residual, adjacency, wq, wk, wv, bq, bk, bv,
                   gain, shift, identity_in, out_features, out_tokens):
    own_queries = query_source is not None
    with ExitStack() as ctx:
        def sb(n, shape, dtype=F32):
            return ctx.enter_context(nc.sbuf_tensor(f"{name}_{n}", shape, dtype))

        def sem(n):
            return ctx.enter_context(nc.semaphore(f"{name}_{n}"))

        def bank(n):
            return ctx.enter_context(nc.psum_tensor(f"{name}_{n}", [P, 512], F32))

        wh = {w: sb(f"w{w}_hi", [P, C, D], F32R) for w in "vkq"}
        wl = {w: sb(f"w{w}_lo", [P, C, D], F32R) for w in "vkq"}
        identity = sb("identity", [P, P])
        bias_q = sb("bias_q", [P, C])
        bias_k = sb("bias_k", [P, C])
        bias_v = sb("bias_v", [P, D])
        gain_row = sb("gain_row", [P, D])
        shift_row = sb("shift_row", [P, D])
        half = sb("minus_half", [P, GB])
        dve_scratch = sb("dve_scratch", [P, 2 + GB])
        pool_scratch = sb("pool_scratch", [P, 4])
        source_raw = sb("source_raw", [P, C, GT])
        source_hi = [sb(f"source_hi{p}", [P, C, GT], F32R) for p in range(2)]
        source_lo = [sb(f"source_lo{p}", [P, C, GT], F32R) for p in range(2)]
        if own_queries:
            query_raw = sb("query_raw", [P, C, GT])
            query_hi = sb("query_hi", [P, C, GT], F32R)
            query_lo = sb("query_lo", [P, C, GT], F32R)
        q_hi = sb("q_hi", [P, GT], F32R)
        q_lo = sb("q_lo", [P, GT], F32R)
        k_hi = sb("k_hi", [P, 2, GT], F32R)
        k_lo = sb("k_lo", [P, 2, GT], F32R)
        v_part = [[sb(f"v{i}_{p}", [P, GB, D], BF16) for i in range(3)] for p in range(2)]
        v_rest = sb("v_rest", [P, 2, D])
        adj = sb("adj", [P, GB, P])
        mask = sb("mask", [P, GB, P])
        probs = sb("probs", [P, UNIT, P])
        minus_max = sb("minus_max", [P, UNIT])
        row_sum = sb("row_sum", [P, UNIT])
        row_inverse = sb("row_inverse", [P, UNIT])
        pt_hi = sb("pt_hi", [P, UNIT, P], F16)
        pt_lo = sb("pt_lo", [P, UNIT, P], F16)
        tokens = sb("tokens", [P, GB, D])
        attended = sb("attended", [P, GB, D])
        normed = sb("normed", [P, GB, D])
        stats = sb("stats", [P, GB, 6])
        moments = sb("moments", [P, GB, 2])
        spread = sb("spread", [P, GB])
        rstd = sb("rstd", [P, GB])
        turned = sb("turned", [P, 2, C, P])

        proj_bank = [bank("proj0"), bank("proj1")]
        score_bank = [bank("score0"), bank("score1")]
        pt_bank = [bank("pt0"), bank("pt1")]
        out_bank = bank("out")
        turn_bank = bank("turn")

        weights_in = {w: sem(f"weight_{w}_in") for w in "vkq"}
        constants_in = sem("constants_in")
        source_in, query_in, adj_in, tokens_in = sem("source_in"), sem("query_in"), sem("adj_in"), sem("tokens_in")
        weight_hi, weight_lo = sem("weight_hi"), sem("weight_lo")
        zeroed = sem("zeroed")
        source_hi_ready, source_ready = sem("source_hi_ready"), sem("source_ready")
        query_hi_ready, query_ready = sem("query_hi_ready"), sem("query_ready")
        projected, proj_hi_ready, proj_split = sem("projected"), sem("proj_hi_ready"), sem("proj_split")
        v_middle_ready, values_ready = sem("v_middle_ready"), sem("values_ready")
        mask_ready = sem("mask_ready")
        scored, masked, exped = sem("scored"), sem("masked"), sem("exped")
        pt_ready, pt_hi_ready, pt_split = sem("pt_ready"), sem("pt_hi_ready"), sem("pt_split")
        weighed, inverted, attended_ready = sem("weighed"), sem("inverted"), sem("attended_ready")
        biased, summed, stats_ready, moments_ready = sem("biased"), sem("summed"), sem("stats_ready"), sem("moments_ready")
        spread_ready, rstd_ready, centred = sem("spread_ready"), sem("rstd_ready"), sem("centred")
        gained, shifted = sem("gained"), sem("shifted")
        turned_ready, turned_copied = sem("turned_ready"), sem("turned_copied")
        turned_out = [sem("turned_out0"), sem("turned_out1")]
        tokens_out = sem("tokens_out")

        weight_raw = {"v": attended, "k": normed, "q": tokens}
        source_view = value_source.rearrange("(c p) t -> p c t", p=P)
        query_view = query_source.rearrange("(c p) t -> p c t", p=P) if own_queries else None
        residual_view = residual.rearrange("(b p) d -> p b d", p=P)
        out_view = out_features.rearrange("(c p) t -> p c t", p=P)
        out_tokens_view = out_tokens.rearrange("(b p) d -> p b d", p=P) if out_tokens is not None else None

        block = ctx.enter_context(nc.Block())

        @block.sync
        def _(sp):
            for w, matrix in (("v", wv), ("k", wk), ("q", wq)):
                sp.dma_start(weight_raw[w][:], matrix.rearrange("(c p) n -> p c n", p=P)).then_inc(weights_in[w], 16)
                if w == "v":
                    sp.dma_start(source_raw[:], source_view[:, :, 0:GT]).then_inc(source_in, 16)
            for tile, data in ((identity[:], identity_in), (bias_q[:], bq), (bias_k[:], bk), (bias_v[:], row(bv)),
                               (gain_row[:], row(gain)), (shift_row[:], row(shift))):
                sp.dma_start(tile, data).then_inc(constants_in, 16)
            sp.dma_start(adj[:], adjacency[:, 0:GB, :]).then_inc(adj_in, 16)
            if own_queries:
                sp.dma_start(query_raw[:], query_view[:, :, 0:GT]).then_inc(query_in, 16)

            def body(g, parity):
                if whole(g):
                    wait(sp, source_ready, C * g + C)
                    sp.dma_start(source_raw[:], source_view[:, :, bass.ds((g + 1) * GT, GT)]).then_inc(source_in, 16)
                    wait(sp, mask_ready, g + 1)
                    sp.dma_start(adj[:], adjacency[:, bass.ds((g + 1) * GB, GB), :]).then_inc(adj_in, 16)
                    if own_queries:
                        wait(sp, query_ready, C * g + C)
                        sp.dma_start(query_raw[:], query_view[:, :, bass.ds((g + 1) * GT, GT)]).then_inc(query_in, 16)
                if not ends(g):
                    wait(sp, summed, GB * g)
                    if starts(g):
                        wait(sp, weight_lo, 3)
                    sp.dma_start(tokens[:], residual_view[:, bass.ds(g * GB, GB), :]).then_inc(tokens_in, 16)
                if not starts(g):
                    for b in range(GB):
                        wait(sp, turned_copied, GB * (g - 1) + b + 1)
                        sp.dma_start(out_view[:, :, bass.ds((g - 1) * GT + b * P, P)], turned[:, b % 2]).then_inc(turned_out[b % 2], 16)
                    if out_tokens is not None:
                        wait(sp, shifted, GB * g)
                        sp.dma_start(out_tokens_view[:, bass.ds((g - 1) * GB, GB), :], normed[:]).then_inc(tokens_out, 16)

            over_groups(sp, body)
            for s in turned_out:
                sp.wait_ge(s, 16 * 2 * NG)
            if out_tokens is not None:
                sp.wait_ge(tokens_out, 16 * NG)

        @block.scalar
        def _(act):
            for n, w in enumerate("vkq"):
                act.wait_ge(weights_in[w], 16)
                nc.scalar.copy(wh[w][:], weight_raw[w][:]).then_inc(weight_hi, 1)
                if w == "v":
                    act.wait_ge(source_in, 16)
                    for c in range(C):
                        nc.scalar.copy(source_hi[0][:, c, :], source_raw[:, c, :]).then_inc(source_hi_ready, 1)
            act.wait_ge(constants_in, 6 * 16)
            act.wait_ge(zeroed, 6)

            def value_high(g, parity, b):
                act.wait_ge(projected, PROJ * g + b + 1)
                nc.scalar.copy(v_part[parity][0][:, b, :], proj_bank[b % 2][:]).then_inc(proj_hi_ready, 1)

            def key_high(g, u):
                act.wait_ge(projected, PROJ * g + GB + 2 * u + 1)
                nc.scalar.activation(k_hi[0:HD, 0, :], proj_bank[0][0:HD, :], ACT.Identity, bias=bias_k[0:HD, u:u + 1])
                nc.scalar.activation(k_hi[HD:P, 1, :], proj_bank[0][HD:P, :], ACT.Identity,
                                     bias=bias_k[HD:P, u:u + 1]).then_inc(proj_hi_ready, 1)

            def query_high(g, u):
                act.wait_ge(projected, PROJ * g + GB + 2 * u + 2)
                nc.scalar.activation(q_hi[:], proj_bank[1][:], ACT.Identity, bias=bias_q[:, u:u + 1]).then_inc(proj_hi_ready, 1)

            def exponentials(g, u):
                for j in range(UNIT):
                    act.wait_ge(masked, UNIT * (C * g + u) + j + 1)
                    nc.scalar.activation(probs[:, j, :], probs[:, j, :], ACT.Exp, bias=minus_max[:, j:j + 1], scale=-1.0,
                                         accum_out=row_sum[:, j:j + 1]).then_inc(exped, 1)

            def transposed_high(g, u, h):
                act.wait_ge(pt_ready, 2 * (C * g + u) + h + 1)
                nc.scalar.copy(pt_hi[:, 4 * h:4 * h + 4, :], pt_bank[h][:].rearrange("p (j i) -> p j i", j=4)).then_inc(pt_hi_ready, 1)

            def copy_turned(g, b):
                act.wait_ge(turned_ready, GB * g + b + 1)
                wait(act, turned_out[b % 2], 16 * (2 * g + b // 2))
                nc.scalar.copy(turned[:, b % 2], turn_bank[:].rearrange("p (c t) -> p c t", c=C)).then_inc(turned_copied, 1)

            def body(g, parity):
                for u in range(C):
                    if u == 0:
                        if not ends(g):
                            value_high(g, parity, 0)
                        if not starts(g):
                            transposed_high(g - 1, C - 1, 0)
                        if not ends(g):
                            value_high(g, parity, 1)
                        if not starts(g):
                            transposed_high(g - 1, C - 1, 1)
                        if not ends(g):
                            value_high(g, parity, 2)
                            if own_queries:
                                act.wait_ge(query_in, 16 * g + 16)
                                wait(act, projected, PROJ * g)
                                for c in range(C):
                                    nc.scalar.copy(query_hi[:, c, :], query_raw[:, c, :]).then_inc(query_hi_ready, 1)
                            value_high(g, parity, 3)
                            key_high(g, 0)
                            query_high(g, 0)
                            exponentials(g, 0)
                        continue
                    if not ends(g):
                        key_high(g, u)
                        transposed_high(g, u - 1, 0)
                        query_high(g, u)
                        transposed_high(g, u - 1, 1)
                    if u == 1 and whole(g):
                        act.wait_ge(source_in, 16 * g + 32)
                        for c in range(C):
                            nc.scalar.copy(source_hi[1 - parity][:, c, :], source_raw[:, c, :]).then_inc(source_hi_ready, 1)
                    if u >= 2 and not starts(g):
                        copy_turned(g - 1, 2 * (u - 2))
                        copy_turned(g - 1, 2 * (u - 2) + 1)
                    if not ends(g):
                        exponentials(g, u)

            over_groups(act, body)

        @block.gpsimd
        def _(pool):
            nc.gpsimd.memset(half[:], -0.5).then_inc(zeroed, 1)
            nc.gpsimd.memset(pool_scratch[:], 0.0).then_inc(zeroed, 1)
            for c in range(C):
                pool.wait_ge(source_hi_ready, c + 1)
                nc.gpsimd.tensor_tensor(source_lo[0][:, c, :], source_raw[:, c, :], source_hi[0][:, c, :].bitcast(F32),
                                        ALU.subtract).then_inc(source_ready, 1)
            pool.wait_ge(constants_in, 6 * 16)
            pool.wait_ge(zeroed, 6)

            def value_low(g, parity, b):
                pool_gate(pool, proj_split, PROJ * g + b + 1, pool_scratch)
                nc.gpsimd.tensor_copy(v_part[parity][1][:, b, :], v_rest[:, b % 2, :]).then_inc(v_middle_ready, 1)
                pool.wait_ge(v_middle_ready, GB * g + b + 1)
                nc.gpsimd.tensor_tensor(v_part[parity][2][:, b, :], v_rest[:, b % 2, :], v_part[parity][1][:, b, :],
                                        ALU.subtract).then_inc(values_ready, 1)

            def body(g, parity):
                if not ends(g):
                    for b in range(GB):
                        value_low(g, parity, b)
                        if b == 2 and own_queries:
                            for c in range(C):
                                pool.wait_ge(query_hi_ready, C * g + c + 1)
                                nc.gpsimd.tensor_tensor(query_lo[:, c, :], query_raw[:, c, :], query_hi[:, c, :].bitcast(F32),
                                                        ALU.subtract).then_inc(query_ready, 1)
                if not starts(g):
                    pool_gate(pool, moments_ready, GB * g, pool_scratch)
                    nc.gpsimd.tensor_scalar(spread[:], moments[:, :, 1], EPS, None, ALU.add).then_inc(spread_ready, 1)
                    pool.wait_ge(spread_ready, g)
                    nc.gpsimd.tensor_tensor(rstd[:], spread[:], half[:], ALU.pow).then_inc(rstd_ready, 1)
                if whole(g):
                    for c in range(C):
                        pool.wait_ge(source_hi_ready, C * g + C + c + 1)
                        nc.gpsimd.tensor_tensor(source_lo[1 - parity][:, c, :], source_raw[:, c, :],
                                                source_hi[1 - parity][:, c, :].bitcast(F32), ALU.subtract).then_inc(source_ready, 1)
                if not starts(g):
                    for b in range(GB):
                        pool.wait_ge(centred, GB * (g - 1) + b + 1)
                        nc.gpsimd.tensor_tensor(normed[:, b, :], normed[:, b, :], gain_row[:], ALU.mult).then_inc(gained, 1)
                        pool.wait_ge(gained, GB * (g - 1) + b + 1)
                        nc.gpsimd.tensor_tensor(normed[:, b, :], normed[:, b, :], shift_row[:], ALU.add).then_inc(shifted, 1)
                if not ends(g):
                    pool.wait_ge(tokens_in, 16 * g + 16)
                    for b in range(GB):
                        nc.gpsimd.tensor_tensor(tokens[:, b, :], tokens[:, b, :], bias_v[:], ALU.add).then_inc(biased, 1)

            over_groups(pool, body)

        @block.vector
        def _(dve):
            nc.vector.memset(k_hi[HD:P, 0, :].bitcast(F32), 0.0).then_inc(zeroed, 1)
            nc.vector.memset(k_hi[0:HD, 1, :].bitcast(F32), 0.0).then_inc(zeroed, 1)
            nc.vector.memset(k_lo[HD:P, 0, :].bitcast(F32), 0.0).then_inc(zeroed, 1)
            nc.vector.memset(k_lo[0:HD, 1, :].bitcast(F32), 0.0).then_inc(zeroed, 1)
            for n, w in enumerate("vkq"):
                dve.wait_ge(weight_hi, n + 1)
                nc.vector.tensor_tensor(wl[w][:], weight_raw[w][:], wh[w][:].bitcast(F32), ALU.subtract).then_inc(weight_lo, 1)
            dve.wait_ge(constants_in, 6 * 16)
            dve.wait_ge(zeroed, 6)

            def value_rest(g, parity, b):
                dve.wait_ge(proj_hi_ready, PROJ * g + b + 1)
                wait(dve, values_ready, GB * g + b - 1)
                nc.vector.tensor_tensor(v_rest[:, b % 2, :], proj_bank[b % 2][:], v_part[parity][0][:, b, :],
                                        ALU.subtract).then_inc(proj_split, 1)

            def key_low(g, u):
                dve.wait_ge(proj_hi_ready, PROJ * g + GB + 2 * u + 1)
                nc.vector.scalar_tensor_tensor(k_lo[0:HD, 0, :], proj_bank[0][0:HD, :], bias_k[0:HD, u:u + 1],
                                               k_hi[0:HD, 0, :].bitcast(F32), ALU.add, ALU.subtract)
                nc.vector.scalar_tensor_tensor(k_lo[HD:P, 1, :], proj_bank[0][HD:P, :], bias_k[HD:P, u:u + 1],
                                               k_hi[HD:P, 1, :].bitcast(F32), ALU.add, ALU.subtract).then_inc(proj_split, 1)

            def query_low(g, u):
                dve.wait_ge(proj_hi_ready, PROJ * g + GB + 2 * u + 2)
                nc.vector.scalar_tensor_tensor(q_lo[:], proj_bank[1][:], bias_q[:, u:u + 1], q_hi[:].bitcast(F32),
                                               ALU.add, ALU.subtract).then_inc(proj_split, 1)

            def mask_and_maximum(g, u):
                if u == 0:
                    dve.wait_ge(mask_ready, g + 1)
                for h in range(2):
                    gate(dve, scored, 2 * (C * g + u) + h + 1, dve_scratch[:, h:h + 1])
                    for j in range(4):
                        nc.vector.tensor_tensor_reduce(
                            out=probs[:, 4 * h + j, :], in0=score_bank[h][:, j * P:(j + 1) * P],
                            in1=mask[:, 2 * h + j // 2, :], scale=-SCALE, scalar=LARGEST, op0=ALU.add, op1=ALU.min,
                            accum_out=minus_max[:, 4 * h + j:4 * h + j + 1]).then_inc(masked, 1)

            def transposed_low(g, u, h):
                dve.wait_ge(pt_hi_ready, 2 * (C * g + u) + h + 1)
                nc.vector.tensor_tensor(pt_lo[:, 4 * h:4 * h + 4, :], pt_bank[h][:].rearrange("p (j i) -> p j i", j=4),
                                        pt_hi[:, 4 * h:4 * h + 4, :], ALU.subtract).then_inc(pt_split, 1)

            def divide(g, u):
                dve.wait_ge(exped, UNIT * (C * g + u + 1))
                nc.vector.reciprocal(row_inverse[:], row_sum[:]).then_inc(inverted, 1)
                dve.wait_ge(inverted, C * g + u + 1)
                dve.wait_ge(weighed, C * g + u + 1)
                nc.vector.tensor_tensor(
                    attended[:, :, u * P:(u + 1) * P].rearrange("p b (h d) -> p b h d", h=2),
                    out_bank[:].rearrange("p (b h d) -> p b h d", b=GB, h=2),
                    row_inverse[:].rearrange("p (b h o) -> p b h o", b=GB, o=1).to_broadcast([P, GB, 2, HD]),
                    ALU.mult).then_inc(attended_ready, 1)

            def sum_and_stats(g, b):
                if b == 0:
                    dve.wait_ge(attended_ready, C * g + C)
                    if out_tokens is not None:
                        wait(dve, tokens_out, 16 * g)
                dve.wait_ge(biased, GB * g + b + 1)
                wait(dve, turned_ready, GB * g)
                nc.vector.tensor_tensor(normed[:, b, :], attended[:, b, :], tokens[:, b, :], ALU.add).then_inc(summed, 1)
                dve.wait_ge(summed, GB * g + b + 1)
                nc.vector.bn_stats(stats[:, b, :], normed[:, b, :]).then_inc(stats_ready, 1)
                gate(dve, stats_ready, GB * g + b + 1, dve_scratch[:, 2 + b:3 + b])
                nc.vector.bn_aggr(moments[:, b, :], stats[:, b, :]).then_inc(moments_ready, 1)

            def centre(g):
                dve.wait_ge(rstd_ready, g + 1)
                for b in range(GB):
                    nc.vector.tensor_scalar(normed[:, b, :], normed[:, b, :], moments[:, b, 0:1], rstd[:, b:b + 1],
                                            ALU.subtract, ALU.mult).then_inc(centred, 1)

            def body(g, parity):
                for u in range(C):
                    if u == 0:
                        if not ends(g):
                            dve.wait_ge(adj_in, 16 * g + 16)
                            wait(dve, masked, UNIT * C * g)
                            nc.vector.tensor_scalar(mask[:], adj[:], 0.0, MASKED, ALU.is_le, ALU.mult).then_inc(mask_ready, 1)
                            value_rest(g, parity, 0)
                        if not starts(g):
                            transposed_low(g - 1, C - 1, 0)
                        if not ends(g):
                            value_rest(g, parity, 1)
                        if not starts(g):
                            transposed_low(g - 1, C - 1, 1)
                            divide(g - 1, C - 1)
                        if not ends(g):
                            value_rest(g, parity, 2)
                        if not starts(g):
                            sum_and_stats(g - 1, 0)
                        if not ends(g):
                            value_rest(g, parity, 3)
                        if not starts(g):
                            sum_and_stats(g - 1, 1)
                        if not ends(g):
                            key_low(g, 0)
                            query_low(g, 0)
                            mask_and_maximum(g, 0)
                        continue
                    if not ends(g):
                        key_low(g, u)
                        transposed_low(g, u - 1, 0)
                    if u == 1 and not starts(g):
                        sum_and_stats(g - 1, 2)
                    if not ends(g):
                        query_low(g, u)
                        transposed_low(g, u - 1, 1)
                    if u == 1 and not starts(g):
                        sum_and_stats(g - 1, 3)
                    if not ends(g):
                        divide(g, u - 1)
                        mask_and_maximum(g, u)
                    if u == 1 and not starts(g):
                        centre(g - 1)

            over_groups(dve, body)

        @block.tensor
        def _(pe):
            pe.wait_ge(constants_in, 6 * 16)
            pe.wait_ge(zeroed, 6)

            def parts(a, b):
                return ((a[0], b[0]), (a[0], b[1]), (a[1], b[0]))

            def project(g, n, products):
                wait(pe, proj_split, PROJ * g + n - 1)
                for i, (stationary, moving) in enumerate(products):
                    last = nc.tensor.matmul(proj_bank[n % 2][:], stationary, moving, start=(i == 0), stop=(i == len(products) - 1))
                last.then_inc(projected, 1)

            def values(g, parity, b):
                if b == 0:
                    pe.wait_ge(source_ready, C * g + C)
                    if starts(g):
                        pe.wait_ge(weight_lo, 1)
                x = [s[parity] for s in (source_hi, source_lo)]
                project(g, b, [(s[:, c, b * P:(b + 1) * P], w[:, c, :]) for c in range(C)
                               for s, w in parts(x, (wh["v"], wl["v"]))])

            def keys(g, parity, u):
                if starts(g) and u == 0:
                    pe.wait_ge(weight_lo, 2)
                x = [s[parity] for s in (source_hi, source_lo)]
                project(g, GB + 2 * u, [(w[:, c, u * P:(u + 1) * P], s[:, c, :]) for c in range(C)
                                        for s, w in parts(x, (wh["k"], wl["k"]))])

            def queries(g, parity, u):
                if u == 0:
                    if own_queries:
                        pe.wait_ge(query_ready, C * g + C)
                    if starts(g):
                        pe.wait_ge(weight_lo, 3)
                x = (query_hi, query_lo) if own_queries else [s[parity] for s in (source_hi, source_lo)]
                project(g, GB + 2 * u + 1, [(w[:, c, u * P:(u + 1) * P], s[:, c, :]) for c in range(C)
                                            for s, w in parts(x, (wh["q"], wl["q"]))])

            def scores(g, u):
                pe.wait_ge(proj_split, PROJ * g + GB + 2 * u + 2)
                for h in range(2):
                    for i in range(2):
                        b = 2 * h + i
                        products = parts([q[:, b * P:(b + 1) * P] for q in (q_hi, q_lo)],
                                         [k[:, :, b * P:(b + 1) * P] for k in (k_hi, k_lo)])
                        for n, (q, k) in enumerate(products):
                            last = nc.tensor.matmul(
                                score_bank[h][:, 2 * i * P:2 * (i + 1) * P].rearrange("p (s j) -> p s j", s=2), q, k,
                                start=(n == 0), stop=(n == 2))
                    last.then_inc(scored, 1)

            def transposes(g, u, h):
                pe.wait_ge(exped, UNIT * (C * g + u) + 4 * (h + 1))
                for j in range(4):
                    last = nc.tensor.transpose(pt_bank[h][:, j * P:(j + 1) * P], probs[:, 4 * h + j, :], identity[:])
                last.then_inc(pt_ready, 1)

            def weigh(g, parity, u):
                if u == 0:
                    pe.wait_ge(values_ready, GB * g + GB)
                wait(pe, attended_ready, C * g + u)
                for h in range(2):
                    pe.wait_ge(pt_split, 2 * (C * g + u) + h + 1)
                    for j in range(4):
                        b, column = 2 * h + j // 2, u * P + (j % 2) * HD
                        v = [part[:, b, column:column + HD] for part in v_part[parity]]
                        hi, lo = pt_hi[:, 4 * h + j, :], pt_lo[:, 4 * h + j, :]
                        out = out_bank[:, (4 * h + j) * HD:(4 * h + j + 1) * HD]
                        products = ((hi, v[0]), (hi, v[1]), (hi, v[2]), (lo, v[0]), (lo, v[1]))
                        for n, (p, value) in enumerate(products):
                            last = nc.tensor.matmul(out, p, value, start=(n == 0), stop=(n == len(products) - 1))
                last.then_inc(weighed, 1)

            def turn(g, b):
                pe.wait_ge(shifted, GB * g + b + 1)
                wait(pe, turned_copied, GB * g + b)
                for c in range(C):
                    last = nc.tensor.transpose(turn_bank[:, c * P:(c + 1) * P], normed[:, b, c * P:(c + 1) * P], identity[:])
                last.then_inc(turned_ready, 1)

            def body(g, parity):
                for u in range(C):
                    if u == 0:
                        if not ends(g):
                            values(g, parity, 0)
                        if not starts(g):
                            transposes(g - 1, C - 1, 0)
                        if not ends(g):
                            values(g, parity, 1)
                        if not starts(g):
                            transposes(g - 1, C - 1, 1)
                            weigh(g - 1, 1 - parity, C - 1)
                        if not ends(g):
                            values(g, parity, 2)
                            values(g, parity, 3)
                            keys(g, parity, 0)
                            queries(g, parity, 0)
                            scores(g, 0)
                        continue
                    if not ends(g):
                        keys(g, parity, u)
                        transposes(g, u - 1, 0)
                        queries(g, parity, u)
                        transposes(g, u - 1, 1)
                    if u >= 2 and not starts(g):
                        turn(g - 1, 2 * (u - 2))
                    if not ends(g):
                        weigh(g, parity, u - 1)
                    if u >= 2 and not starts(g):
                        turn(g - 1, 2 * (u - 2) + 1)
                    if not ends(g):
                        scores(g, u)

            over_groups(pe, body)


def feed_forward_pass(nc, source, nodes, x, w1, b1, w2, b2, gain, shift, out):
    name = "ffn"
    with ExitStack() as ctx:
        def sb(n, shape, dtype=F32):
            return ctx.enter_context(nc.sbuf_tensor(f"{name}_{n}", shape, dtype))

        def sem(n):
            return ctx.enter_context(nc.semaphore(f"{name}_{n}"))

        def bank(n):
            return ctx.enter_context(nc.psum_tensor(f"{name}_{n}", [P, 512], F32))

        w1_hi, w1_lo = (sb(f"w1_{s}", [P, C, FF], F32R) for s in ("hi", "lo"))
        w2_hi, w2_lo = (sb(f"w2_{s}", [P, FC, D], F32R) for s in ("hi", "lo"))
        bias_1 = sb("bias_1", [P, FC])
        bias_2 = sb("bias_2", [P, D])
        gain_row = sb("gain_row", [P, D])
        shift_row = sb("shift_row", [P, D])
        half = sb("minus_half", [P, GB])
        dve_scratch = sb("dve_scratch", [P, 2 + GB])
        pool_scratch = sb("pool_scratch", [P, 4])
        source_raw = sb("source_raw", [P, C, GT])
        source_hi = [sb(f"source_hi{p}", [P, C, GT], F32R) for p in range(2)]
        source_lo = [sb(f"source_lo{p}", [P, C, GT], F32R) for p in range(2)]
        hidden = sb("hidden", [P, 2, GT])
        hidden_hi = sb("hidden_hi", [P, 2, GT], F32R)
        hidden_lo = sb("hidden_lo", [P, 2, GT], F32R)
        tokens = sb("tokens", [P, GB, D])
        x_tile = sb("x_tile", [P, 2, D])
        stats = sb("stats", [P, GB, 6])
        moments = sb("moments", [P, GB, 2])
        spread = sb("spread", [P, GB])
        rstd = sb("rstd", [P, GB])

        up_bank = [bank(f"up{i}") for i in range(2)]
        down_bank = [bank(f"down{i}") for i in range(GB)]

        NW = 8
        weights_in = [sem(f"weights_in{i}") for i in range(2)]
        constants_in, source_in, tokens_in = sem("constants_in"), sem("source_in"), sem("tokens_in")
        x_in = [sem("x_in0"), sem("x_in1")]
        zeroed, weight_hi, weight_lo = sem("zeroed"), sem("weight_hi"), sem("weight_lo")
        source_hi_ready, source_ready = sem("source_hi_ready"), sem("source_ready")
        raised, activated, hidden_hi_ready, hidden_ready = sem("raised"), sem("activated"), sem("hidden_hi_ready"), sem("hidden_ready")
        lowered, biased, summed = sem("lowered"), sem("biased"), sem("summed")
        stats_ready, moments_ready = sem("stats_ready"), sem("moments_ready")
        spread_ready, rstd_ready, centred = sem("spread_ready"), sem("rstd_ready"), sem("centred")
        gained, shifted, topped = sem("gained"), sem("shifted"), sem("topped")
        stored = sem("stored")

        source_view = source.rearrange("(c p) t -> p c t", p=P)
        nodes_view = nodes.rearrange("(b p) d -> p b d", p=P)
        x_view = x.rearrange("(b p) d -> p b d", p=P)
        out_view = out.rearrange("(b p) d -> p b d", p=P)
        w1_view = w1.rearrange("(c p) n -> p c n", p=P)
        w2_view = w2.rearrange("(c p) n -> p c n", p=P)
        weight_raw = [tokens, source_raw]
        weight_parts = ([(w1_view[:, :, n * D:(n + 1) * D], w1_hi[:, :, n * D:(n + 1) * D], w1_lo[:, :, n * D:(n + 1) * D])
                         for n in range(4)]
                        + [(w2_view[:, n * C:(n + 1) * C, :], w2_hi[:, n * C:(n + 1) * C, :], w2_lo[:, n * C:(n + 1) * C, :])
                           for n in range(4)])

        block = ctx.enter_context(nc.Block())

        @block.sync
        def _(sp):
            for n, (matrix, _, _) in enumerate(weight_parts):
                wait(sp, weight_lo, n - 1)
                sp.dma_start(weight_raw[n % 2][:], matrix).then_inc(weights_in[n % 2], 16)
            for tile, data in ((bias_1[:], b1), (bias_2[:], row(b2)), (gain_row[:], row(gain)), (shift_row[:], row(shift))):
                sp.dma_start(tile, data).then_inc(constants_in, 16)
            sp.wait_ge(weight_lo, NW)
            sp.dma_start(source_raw[:], source_view[:, :, 0:GT]).then_inc(source_in, 16)

            def body(g, parity):
                if whole(g):
                    wait(sp, source_ready, C * g + C)
                    sp.dma_start(source_raw[:], source_view[:, :, bass.ds((g + 1) * GT, GT)]).then_inc(source_in, 16)
                if not starts(g):
                    for b in range(GB):
                        n = GB * (g - 1) + b
                        if b >= 2:
                            sp.wait_ge(topped, GB * (g - 1) + b - 1)
                        sp.dma_start(x_tile[:, b % 2, :], x_view[:, (g - 1) * GB + b, :] if isinstance(g, int)
                                     else x_view[:, bass.ds((g - 1) * GB + b, 1), :].rearrange("p b d -> p (b d)")).then_inc(x_in[b % 2], 16)
                    wait(sp, centred, 2 * GB * g)
                    sp.dma_start(out_view[:, bass.ds((g - 1) * GB, GB), :], tokens[:]).then_inc(stored, 16)
                if not ends(g):
                    wait(sp, stored, 16 * g)
                    sp.dma_start(tokens[:], nodes_view[:, bass.ds(g * GB, GB), :]).then_inc(tokens_in, 16)

            over_groups(sp, body)
            sp.wait_ge(stored, 16 * NG)

        @block.scalar
        def _(act):
            for n, (_, hi, _) in enumerate(weight_parts):
                act.wait_ge(weights_in[n % 2], 16 * (n // 2 + 1))
                nc.scalar.copy(hi, weight_raw[n % 2][:]).then_inc(weight_hi, 1)
            act.wait_ge(source_in, 16)
            for c in range(C):
                nc.scalar.copy(source_hi[0][:, c, :], source_raw[:, c, :]).then_inc(source_hi_ready, 1)
            act.wait_ge(constants_in, 4 * 16)

            def hidden_high(g, c):
                act.wait_ge(activated, FC * g + c + 1)
                nc.scalar.copy(hidden_hi[:, c % 2, :], hidden[:, c % 2, :]).then_inc(hidden_hi_ready, 1)

            def body(g, parity):
                for c in range(FC):
                    if not ends(g):
                        act.wait_ge(raised, FC * g + c + 1)
                        wait(act, hidden_ready, FC * g + c - 1)
                        nc.scalar.activation(hidden[:, c % 2, :], up_bank[c % 2][:], ACT.Gelu,
                                             bias=bias_1[:, c:c + 1]).then_inc(activated, 1)
                        hidden_high(g, c)
                    if 8 <= c < 8 + C and whole(g):
                        if c == 8:
                            act.wait_ge(source_in, 16 * g + 32)
                        nc.scalar.copy(source_hi[1 - parity][:, c - 8, :], source_raw[:, c - 8, :]).then_inc(source_hi_ready, 1)

            over_groups(act, body)

        @block.gpsimd
        def _(pool):
            nc.gpsimd.memset(half[:], -0.5).then_inc(zeroed, 1)
            nc.gpsimd.memset(pool_scratch[:], 0.0).then_inc(zeroed, 1)
            pool.wait_ge(zeroed, 2)
            for c in range(C):
                pool.wait_ge(source_hi_ready, c + 1)
                nc.gpsimd.tensor_tensor(source_lo[0][:, c, :], source_raw[:, c, :], source_hi[0][:, c, :].bitcast(F32),
                                        ALU.subtract).then_inc(source_ready, 1)
            pool.wait_ge(constants_in, 4 * 16)

            def inverse_spread(g, norm):
                n = 2 * g + norm
                pool_gate(pool, moments_ready, GB * (n + 1), pool_scratch)
                nc.gpsimd.tensor_scalar(spread[:], moments[:, :, 1], EPS, None, ALU.add).then_inc(spread_ready, 1)
                pool.wait_ge(spread_ready, n + 1)
                nc.gpsimd.tensor_tensor(rstd[:], spread[:], half[:], ALU.pow).then_inc(rstd_ready, 1)

            def body(g, parity):
                if not starts(g):
                    inverse_spread(g - 1, 0)
                    for b in range(GB):
                        n = GB * (g - 1) + b + 1
                        pool.wait_ge(centred, 2 * GB * (g - 1) + b + 1)
                        nc.gpsimd.tensor_tensor(tokens[:, b, :], tokens[:, b, :], gain_row[:], ALU.mult).then_inc(gained, 1)
                        pool.wait_ge(gained, n)
                        nc.gpsimd.tensor_tensor(tokens[:, b, :], tokens[:, b, :], shift_row[:], ALU.add).then_inc(shifted, 1)
                        pool.wait_ge(shifted, n)
                        pool.wait_ge(x_in[b % 2], 16 * (2 * (g - 1) + b // 2 + 1))
                        nc.gpsimd.tensor_tensor(tokens[:, b, :], tokens[:, b, :], x_tile[:, b % 2, :], ALU.add).then_inc(topped, 1)
                    inverse_spread(g - 1, 1)
                if whole(g):
                    for c in range(C):
                        pool.wait_ge(source_hi_ready, C * g + C + c + 1)
                        nc.gpsimd.tensor_tensor(source_lo[1 - parity][:, c, :], source_raw[:, c, :],
                                                source_hi[1 - parity][:, c, :].bitcast(F32), ALU.subtract).then_inc(source_ready, 1)
                if not ends(g):
                    pool.wait_ge(tokens_in, 16 * g + 16)
                    for b in range(GB):
                        nc.gpsimd.tensor_tensor(tokens[:, b, :], tokens[:, b, :], bias_2[:], ALU.add).then_inc(biased, 1)

            over_groups(pool, body)

        @block.vector
        def _(dve):
            for n, (_, hi, lo) in enumerate(weight_parts):
                dve.wait_ge(weight_hi, n + 1)
                nc.vector.tensor_tensor(lo, weight_raw[n % 2][:], hi.bitcast(F32), ALU.subtract).then_inc(weight_lo, 1)

            def moments_of(g, norm, b):
                n = 2 * GB * g + GB * norm + b + 1
                nc.vector.bn_stats(stats[:, b, :], tokens[:, b, :]).then_inc(stats_ready, 1)
                gate(dve, stats_ready, n, dve_scratch[:, b:b + 1])
                nc.vector.bn_aggr(moments[:, b, :], stats[:, b, :]).then_inc(moments_ready, 1)

            def centre(g, norm):
                dve.wait_ge(rstd_ready, 2 * g + norm + 1)
                for b in range(GB):
                    nc.vector.tensor_scalar(tokens[:, b, :], tokens[:, b, :], moments[:, b, 0:1], rstd[:, b:b + 1],
                                            ALU.subtract, ALU.mult).then_inc(centred, 1)

            def body(g, parity):
                for c in range(FC):
                    if not ends(g):
                        dve.wait_ge(hidden_hi_ready, FC * g + c + 1)
                        nc.vector.tensor_tensor(hidden_lo[:, c % 2, :], hidden[:, c % 2, :], hidden_hi[:, c % 2, :].bitcast(F32),
                                                ALU.subtract).then_inc(hidden_ready, 1)
                    if starts(g):
                        continue
                    if c == 0:
                        for b in range(GB):
                            dve.wait_ge(lowered, GB * (g - 1) + b + 1)
                            dve.wait_ge(biased, GB * (g - 1) + b + 1)
                            nc.vector.tensor_tensor(tokens[:, b, :], down_bank[b][:], tokens[:, b, :], ALU.add).then_inc(summed, 1)
                    if 2 <= c < 2 + GB:
                        b = c - 2
                        dve.wait_ge(summed, GB * (g - 1) + b + 1)
                        moments_of(g - 1, 0, b)
                    if c == 7:
                        centre(g - 1, 0)
                    if c == 11:
                        for b in range(GB):
                            dve.wait_ge(topped, GB * (g - 1) + b + 1)
                            moments_of(g - 1, 1, b)
                    if c == 13:
                        centre(g - 1, 1)

            over_groups(dve, body)

        @block.tensor
        def _(pe):
            pe.wait_ge(weight_lo, NW)

            def parts(a, b):
                return ((a[0], b[0]), (a[0], b[1]), (a[1], b[0]))

            def up(g, parity, c):
                if c == 0:
                    pe.wait_ge(source_ready, C * g + C)
                wait(pe, activated, FC * g + c - 1)
                products = [p for k in range(C)
                            for p in parts([w[:, k, c * P:(c + 1) * P] for w in (w1_hi, w1_lo)],
                                           [s[parity][:, k, :] for s in (source_hi, source_lo)])]
                for i, (w, s) in enumerate(products):
                    last = nc.tensor.matmul(up_bank[c % 2][:], w, s, start=(i == 0), stop=(i == len(products) - 1))
                last.then_inc(raised, 1)

            def down(g, c):
                pe.wait_ge(hidden_ready, FC * g + c + 1)
                if c == 0:
                    wait(pe, summed, GB * g)
                for b in range(GB):
                    products = parts([h[:, c % 2, b * P:(b + 1) * P] for h in (hidden_hi, hidden_lo)],
                                     [w[:, c, :] for w in (w2_hi, w2_lo)])
                    for i, (h, w) in enumerate(products):
                        last = nc.tensor.matmul(down_bank[b][:], h, w, start=(c == 0 and i == 0), stop=(c == FC - 1 and i == 2))
                    if c == FC - 1:
                        last.then_inc(lowered, 1)

            def body(g, parity):
                for c in range(FC):
                    if not ends(g):
                        up(g, parity, c)
                    if c > 0 and not ends(g):
                        down(g, c - 1)
                    if c == 0 and not starts(g):
                        down(g - 1, FC - 1)

            over_groups(pe, body)


def build(nc, xt, x, adj_t, adj, ident, n2e, e2n, ffn, scratch, out):
    attention_pass(nc, "n2e", None, xt, x, adj_t, *n2e, ident, scratch["edges_t"], None)
    attention_pass(nc, "e2n", xt, scratch["edges_t"], x, adj, *e2n, ident, scratch["nodes_t"], scratch["nodes"])
    feed_forward_pass(nc, scratch["nodes_t"], scratch["nodes"], x, *ffn, out)


def kernel(**inputs):
    import numpy as np
    import concourse.bacc as bacc
    from concourse.bass_utils import run_bass_kernel_spmd

    def weights_t(name):
        return np.ascontiguousarray(np.asarray(inputs["L0_gnn_" + name]).T)

    def vector(name):
        return np.ascontiguousarray(inputs["L0_gnn_" + name])

    def columns(name):
        return np.ascontiguousarray(vector(name).reshape(-1, P).T)

    x = np.ascontiguousarray(inputs["x"]).reshape(T, D)
    adj = np.asarray(inputs["adj"])
    arrays = {
        "x": x,
        "x_t": np.ascontiguousarray(x.T),
        "adj_nodes": np.ascontiguousarray(adj.transpose(1, 0, 2)),
        "adj_edges": np.ascontiguousarray(adj.transpose(2, 0, 1)),
        "identity": np.eye(P, dtype=np.float32),
    }
    for side, norm in (("n2e", "norm1"), ("e2n", "norm2")):
        for p in "qkv":
            arrays[f"{side}_{p}_w"] = weights_t(f"{side}_{p}_w")
        for p in "qk":
            arrays[f"{side}_{p}_b"] = columns(f"{side}_{p}_b")
        arrays[f"{side}_v_b"] = vector(f"{side}_v_b")
        for p in "gb":
            arrays[f"{side}_norm_{p}"] = vector(f"{norm}_{p}")
    arrays |= {"w1": weights_t("ffn_w1"), "b1": columns("ffn_b1"), "w2": weights_t("ffn_w2"), "b2": vector("ffn_b2"),
               "norm_g": vector("norm3_g"), "norm_b": vector("norm3_b")}

    nc = bacc.Bacc("TRN2", target_bir_lowering=False, num_devices=1)
    a = {}
    for name, array in arrays.items():
        a[name] = nc.dram_tensor(f"in_{name}", array.shape, mybir.dt.from_np(array.dtype), kind="ExternalInput").ap()
    out = nc.dram_tensor("out", (T, D), F32, kind="ExternalOutput").ap()
    scratch = {"edges_t": nc.dram_tensor("edges_t", (D, T), F32).ap(),
               "nodes_t": nc.dram_tensor("nodes_t", (D, T), F32).ap(),
               "nodes": nc.dram_tensor("nodes", (T, D), F32).ap()}

    def side(s):
        return tuple(a[f"{s}_{n}"] for n in ("q_w", "k_w", "v_w", "q_b", "k_b", "v_b", "norm_g", "norm_b"))

    build(nc, a["x_t"], a["x"], a["adj_edges"], a["adj_nodes"], a["identity"], side("n2e"), side("e2n"),
          (a["w1"], a["b1"], a["w2"], a["b2"], a["norm_g"], a["norm_b"]), scratch, out)
    result = run_bass_kernel_spmd(nc, [{f"in_{n}": v for n, v in arrays.items()}], core_ids=[0])
    return result.results[0]["out"].reshape(B, P, D)
```

```python
from contextlib import ExitStack

import concourse.bass as bass
from concourse import mybir

P = 128
D = 512
C = D // P
B = 64
T = B * P
GB = 4
GT = GB * P
NG = B // GB
H = 8
HD = D // H
FF = 4 * D
FC = FF // P
SCALE = float(HD) ** -0.5
EPS = 1e-5
MASKED = -1e30
LARGEST = 3e38

F32 = mybir.dt.float32
F32R = mybir.dt.float32r
F16 = mybir.dt.float16
BF16 = mybir.dt.bfloat16
ALU = mybir.AluOpType
ACT = mybir.ActivationFunctionType

PROJ = GB + 2 * C
UNIT = GB * 2


def wait(engine, semaphore, value):
    if isinstance(value, int) and value <= 0:
        return
    engine.wait_ge(semaphore, value)


def gate(engine, semaphore, value, scratch):
    if not isinstance(value, int):
        engine.wait_ge(semaphore, value)
        engine.memset(scratch, 0.0)
    else:
        engine.wait_ge(semaphore, value)


def pool_gate(engine, semaphore, value, scratch):
    engine.wait_ge(semaphore, value)
    if not isinstance(value, int):
        engine.tensor_tensor(scratch[:, 0:1], scratch[:, 1:2], scratch[:, 2:3], ALU.add)


def over_groups(engine, body):
    body(0, 0)
    body(1, 1)
    with engine.Fori(1, NG // 2 - 1) as i:
        body(2 * i, 0)
        body(2 * i + 1, 1)
    body(NG - 2, 0)
    body(NG - 1, 1)
    body(NG, 0)


def starts(group):
    return isinstance(group, int) and group == 0


def ends(group):
    return isinstance(group, int) and group == NG


def whole(group):
    return not (isinstance(group, int) and group >= NG - 1)


def row(vector):
    return vector.rearrange("(a d) -> a d", a=1).to_broadcast([P, D])


def attention_pass(nc, name, query_source, value_source, residual, adjacency, wq, wk, wv, bq, bk, bv,
                   gain, shift, identity_in, out_features, out_tokens):
    own_queries = query_source is not None
    with ExitStack() as ctx:
        def sb(n, shape, dtype=F32):
            return ctx.enter_context(nc.sbuf_tensor(f"{name}_{n}", shape, dtype))

        def sem(n):
            return ctx.enter_context(nc.semaphore(f"{name}_{n}"))

        def bank(n):
            return ctx.enter_context(nc.psum_tensor(f"{name}_{n}", [P, 512], F32))

        wh = {w: sb(f"w{w}_hi", [P, C, D], F32R) for w in "vkq"}
        wl = {w: sb(f"w{w}_lo", [P, C, D], F32R) for w in "vkq"}
        identity = sb("identity", [P, P])
        bias_q = sb("bias_q", [P, C])
        bias_k = sb("bias_k", [P, C])
        bias_v = sb("bias_v", [P, D])
        gain_row = sb("gain_row", [P, D])
        shift_row = sb("shift_row", [P, D])
        half = sb("minus_half", [P, GB])
        dve_scratch = sb("dve_scratch", [P, 2 + GB])
        pool_scratch = sb("pool_scratch", [P, 4])
        source_raw = sb("source_raw", [P, C, GT])
        source_hi = [sb(f"source_hi{p}", [P, C, GT], F32R) for p in range(2)]
        source_lo = [sb(f"source_lo{p}", [P, C, GT], F32R) for p in range(2)]
        if own_queries:
            query_raw = sb("query_raw", [P, C, GT])
            query_hi = sb("query_hi", [P, C, GT], F32R)
            query_lo = sb("query_lo", [P, C, GT], F32R)
        q_hi = sb("q_hi", [P, GT], F32R)
        q_lo = sb("q_lo", [P, GT], F32R)
        k_hi = sb("k_hi", [P, 2, GT], F32R)
        k_lo = sb("k_lo", [P, 2, GT], F32R)
        v_part = [[sb(f"v{i}_{p}", [P, GB, D], BF16) for i in range(3)] for p in range(2)]
        v_rest = sb("v_rest", [P, 2, D])
        adj = sb("adj", [P, GB, P])
        mask = sb("mask", [P, GB, P])
        probs = sb("probs", [P, UNIT, P])
        minus_max = sb("minus_max", [P, UNIT])
        row_sum = sb("row_sum", [P, 2, UNIT])
        row_inverse = sb("row_inverse", [P, 2, UNIT])
        pt_hi = sb("pt_hi", [P, UNIT, P], F16)
        pt_lo = sb("pt_lo", [P, UNIT, P], F16)
        tokens = sb("tokens", [P, GB, D])
        attended = sb("attended", [P, GB, D])
        normed = sb("normed", [P, GB, D])
        stats = sb("stats", [P, GB, 6])
        moments = sb("moments", [P, GB, 2])
        spread = sb("spread", [P, GB])
        rstd = sb("rstd", [P, GB])
        turned = sb("turned", [P, 2, C, P])

        proj_bank = [bank("proj0"), bank("proj1")]
        score_bank = [bank("score0"), bank("score1")]
        pt_bank = [bank("pt0"), bank("pt1")]
        out_bank = bank("out")
        turn_bank = bank("turn")

        weights_in = {w: sem(f"weight_{w}_in") for w in "vkq"}
        constants_in, rows_in = sem("constants_in"), sem("rows_in")
        source_in, query_in, adj_in, tokens_in = sem("source_in"), sem("query_in"), sem("adj_in"), sem("tokens_in")
        weight_hi, weight_lo = sem("weight_hi"), sem("weight_lo")
        zeroed = sem("zeroed")
        source_hi_ready, source_ready = sem("source_hi_ready"), sem("source_ready")
        query_hi_ready, query_ready = sem("query_hi_ready"), sem("query_ready")
        projected, proj_hi_ready, proj_split = sem("projected"), sem("proj_hi_ready"), sem("proj_split")
        v_middle_ready, values_ready = sem("v_middle_ready"), sem("values_ready")
        mask_ready = sem("mask_ready")
        scored, masked, exped = sem("scored"), sem("masked"), sem("exped")
        pt_ready, pt_hi_ready, pt_split = sem("pt_ready"), sem("pt_hi_ready"), sem("pt_split")
        weighed, inverted, attended_ready = sem("weighed"), sem("inverted"), sem("attended_ready")
        biased, summed, stats_ready, moments_ready = sem("biased"), sem("summed"), sem("stats_ready"), sem("moments_ready")
        spread_ready, rstd_ready, centred = sem("spread_ready"), sem("rstd_ready"), sem("centred")
        gained, shifted = sem("gained"), sem("shifted")
        turned_ready, turned_copied = sem("turned_ready"), sem("turned_copied")
        turned_out = [sem("turned_out0"), sem("turned_out1")]
        tokens_out = sem("tokens_out")

        weight_raw = {"v": attended, "k": normed, "q": tokens}
        source_view = value_source.rearrange("(c p) t -> p c t", p=P)
        query_view = query_source.rearrange("(c p) t -> p c t", p=P) if own_queries else None
        residual_view = residual.rearrange("(b p) d -> p b d", p=P)
        out_view = out_features.rearrange("(c p) t -> p c t", p=P)
        out_tokens_view = out_tokens.rearrange("(b p) d -> p b d", p=P) if out_tokens is not None else None

        block = ctx.enter_context(nc.Block())

        @block.sync
        def _(sp):
            sp.dma_start(source_raw[:], source_view[:, :, 0:GT]).then_inc(source_in, 16)
            for w, matrix in (("v", wv), ("k", wk), ("q", wq)):
                sp.dma_start(weight_raw[w][:], matrix.rearrange("(c p) n -> p c n", p=P)).then_inc(weights_in[w], 16)
                if w == "v":
                    for tile, data in ((identity[:], identity_in), (bias_q[:], bq), (bias_k[:], bk)):
                        sp.dma_start(tile, data).then_inc(constants_in, 16)
                    sp.dma_start(adj[:], adjacency[:, 0:GB, :]).then_inc(adj_in, 16)
                if w == "k" and own_queries:
                    sp.dma_start(query_raw[:], query_view[:, :, 0:GT]).then_inc(query_in, 16)
            for tile, data in ((bias_v[:], row(bv)), (gain_row[:], row(gain)), (shift_row[:], row(shift))):
                sp.dma_start(tile, data).then_inc(rows_in, 16)

            def body(g, parity):
                if whole(g):
                    wait(sp, source_ready, C * g + C)
                    sp.dma_start(source_raw[:], source_view[:, :, bass.ds((g + 1) * GT, GT)]).then_inc(source_in, 16)
                    wait(sp, mask_ready, g + 1)
                    sp.dma_start(adj[:], adjacency[:, bass.ds((g + 1) * GB, GB), :]).then_inc(adj_in, 16)
                    if own_queries:
                        wait(sp, query_ready, C * g + C)
                        sp.dma_start(query_raw[:], query_view[:, :, bass.ds((g + 1) * GT, GT)]).then_inc(query_in, 16)
                if not ends(g):
                    wait(sp, summed, GB * g)
                    if starts(g):
                        wait(sp, weight_lo, 3 * C)
                    sp.dma_start(tokens[:], residual_view[:, bass.ds(g * GB, GB), :]).then_inc(tokens_in, 16)
                if not starts(g):
                    for b in range(GB):
                        wait(sp, turned_copied, GB * (g - 1) + b + 1)
                        sp.dma_start(out_view[:, :, bass.ds((g - 1) * GT + b * P, P)], turned[:, b % 2]).then_inc(turned_out[b % 2], 16)
                    if out_tokens is not None:
                        wait(sp, shifted, GB * g)
                        sp.dma_start(out_tokens_view[:, bass.ds((g - 1) * GB, GB), :], normed[:]).then_inc(tokens_out, 16)

            over_groups(sp, body)
            for s in turned_out:
                sp.wait_ge(s, 16 * 2 * NG)
            if out_tokens is not None:
                sp.wait_ge(tokens_out, 16 * NG)

        @block.scalar
        def _(act):
            act.wait_ge(source_in, 16)
            for c in range(C):
                nc.scalar.copy(source_hi[0][:, c, :], source_raw[:, c, :]).then_inc(source_hi_ready, 1)
            for n, w in enumerate("vkq"):
                act.wait_ge(weights_in[w], 16)
                for c in range(C):
                    nc.scalar.copy(wh[w][:, c, :], weight_raw[w][:, c, :]).then_inc(weight_hi, 1)
            act.wait_ge(constants_in, 3 * 16)
            act.wait_ge(zeroed, 6)

            def value_high(g, parity, b):
                act.wait_ge(projected, PROJ * g + b + 1)
                nc.scalar.copy(v_part[parity][0][:, b, :], proj_bank[b % 2][:]).then_inc(proj_hi_ready, 1)

            def key_high(g, u):
                act.wait_ge(projected, PROJ * g + GB + 2 * u + 1)
                nc.scalar.activation(k_hi[0:HD, 0, :], proj_bank[0][0:HD, :], ACT.Identity, bias=bias_k[0:HD, u:u + 1])
                nc.scalar.activation(k_hi[HD:P, 1, :], proj_bank[0][HD:P, :], ACT.Identity,
                                     bias=bias_k[HD:P, u:u + 1]).then_inc(proj_hi_ready, 1)

            def query_high(g, u):
                act.wait_ge(projected, PROJ * g + GB + 2 * u + 2)
                nc.scalar.activation(q_hi[:], proj_bank[1][:], ACT.Identity, bias=bias_q[:, u:u + 1]).then_inc(proj_hi_ready, 1)

            def exponentials(g, u):
                for j in range(UNIT):
                    act.wait_ge(masked, UNIT * (C * g + u) + j + 1)
                    nc.scalar.activation(probs[:, j, :], probs[:, j, :], ACT.Exp, bias=minus_max[:, j:j + 1], scale=-1.0,
                                         accum_out=row_sum[:, u % 2, j:j + 1]).then_inc(exped, 1)

            def transposed_high(g, u, h):
                act.wait_ge(pt_ready, 2 * (C * g + u) + h + 1)
                nc.scalar.copy(pt_hi[:, 4 * h:4 * h + 4, :], pt_bank[h][:].rearrange("p (j i) -> p j i", j=4)).then_inc(pt_hi_ready, 1)

            def copy_turned(g, b):
                act.wait_ge(turned_ready, GB * g + b + 1)
                wait(act, turned_out[b % 2], 16 * (2 * g + b // 2))
                nc.scalar.copy(turned[:, b % 2], turn_bank[:].rearrange("p (c t) -> p c t", c=C)).then_inc(turned_copied, 1)

            def split_queries(g, chunks):
                if not own_queries or ends(g):
                    return
                if chunks[0] == 0:
                    act.wait_ge(query_in, 16 * g + 16)
                    wait(act, projected, PROJ * g)
                for c in chunks:
                    nc.scalar.copy(query_hi[:, c, :], query_raw[:, c, :]).then_inc(query_hi_ready, 1)

            def split_source(g, parity, chunks):
                if not whole(g):
                    return
                if chunks[0] == 0:
                    act.wait_ge(source_in, 16 * g + 32)
                for c in chunks:
                    nc.scalar.copy(source_hi[1 - parity][:, c, :], source_raw[:, c, :]).then_inc(source_hi_ready, 1)

            def body(g, parity):
                for b in range(2):
                    if not ends(g):
                        value_high(g, parity, b)
                    if not starts(g):
                        transposed_high(g - 1, C - 1, b)
                    split_queries(g, range(2 * b, 2 * b + 2))
                if not ends(g):
                    value_high(g, parity, 2)
                    value_high(g, parity, 3)
                    key_high(g, 0)
                    query_high(g, 0)
                    exponentials(g, 0)
                for u in range(1, C):
                    turning = u == C - 1 and not starts(g)
                    if turning:
                        copy_turned(g - 1, 0)
                    if not ends(g):
                        transposed_high(g, u - 1, 0)
                        key_high(g, u)
                        query_high(g, u)
                        transposed_high(g, u - 1, 1)
                    if u == 1:
                        split_source(g, parity, range(0, 2))
                    if u == 2:
                        split_source(g, parity, range(2, 4))
                    if turning:
                        copy_turned(g - 1, 1)
                        copy_turned(g - 1, 2)
                    if not ends(g):
                        exponentials(g, u)
                    if turning:
                        copy_turned(g - 1, 3)

            over_groups(act, body)

        @block.gpsimd
        def _(pool):
            nc.gpsimd.memset(half[:], -0.5).then_inc(zeroed, 1)
            nc.gpsimd.memset(pool_scratch[:], 0.0).then_inc(zeroed, 1)
            pool.wait_ge(zeroed, 6)

            def value_low(g, parity, b):
                pool_gate(pool, proj_split, PROJ * g + b + 1, pool_scratch)
                nc.gpsimd.tensor_copy(v_part[parity][1][:, b, :], v_rest[:, b % 2, :]).then_inc(v_middle_ready, 1)
                pool.wait_ge(v_middle_ready, GB * g + b + 1)
                nc.gpsimd.tensor_tensor(v_part[parity][2][:, b, :], v_rest[:, b % 2, :], v_part[parity][1][:, b, :],
                                        ALU.subtract).then_inc(values_ready, 1)

            def split_source(g, parity, chunks):
                if not whole(g):
                    return
                for c in chunks:
                    pool.wait_ge(source_hi_ready, C * g + C + c + 1)
                    nc.gpsimd.tensor_tensor(source_lo[1 - parity][:, c, :], source_raw[:, c, :],
                                            source_hi[1 - parity][:, c, :].bitcast(F32), ALU.subtract).then_inc(source_ready, 1)

            def body(g, parity):
                if not ends(g):
                    for b in range(GB):
                        value_low(g, parity, b)
                        if b < 2 and own_queries:
                            for c in range(2 * b, 2 * b + 2):
                                pool.wait_ge(query_hi_ready, C * g + c + 1)
                                nc.gpsimd.tensor_tensor(query_lo[:, c, :], query_raw[:, c, :], query_hi[:, c, :].bitcast(F32),
                                                        ALU.subtract).then_inc(query_ready, 1)
                if not starts(g):
                    pool_gate(pool, moments_ready, GB * g, pool_scratch)
                    nc.gpsimd.tensor_scalar(spread[:], moments[:, :, 1], EPS, None, ALU.add).then_inc(spread_ready, 1)
                    pool.wait_ge(spread_ready, g)
                    nc.gpsimd.tensor_tensor(rstd[:], spread[:], half[:], ALU.pow).then_inc(rstd_ready, 1)
                split_source(g, parity, range(0, 2))
                if not starts(g):
                    for b in range(GB):
                        pool.wait_ge(centred, GB * (g - 1) + b + 1)
                        nc.gpsimd.tensor_tensor(normed[:, b, :], normed[:, b, :], gain_row[:], ALU.mult).then_inc(gained, 1)
                        pool.wait_ge(gained, GB * (g - 1) + b + 1)
                        nc.gpsimd.tensor_tensor(normed[:, b, :], normed[:, b, :], shift_row[:], ALU.add).then_inc(shifted, 1)
                split_source(g, parity, range(2, 4))
                if not ends(g):
                    if starts(g):
                        pool.wait_ge(rows_in, 3 * 16)
                    pool.wait_ge(tokens_in, 16 * g + 16)
                    for b in range(GB):
                        nc.gpsimd.tensor_tensor(tokens[:, b, :], tokens[:, b, :], bias_v[:], ALU.add).then_inc(biased, 1)

            over_groups(pool, body)

        @block.vector
        def _(dve):
            nc.vector.memset(k_hi[HD:P, 0, :].bitcast(F32), 0.0).then_inc(zeroed, 1)
            nc.vector.memset(k_hi[0:HD, 1, :].bitcast(F32), 0.0).then_inc(zeroed, 1)
            nc.vector.memset(k_lo[HD:P, 0, :].bitcast(F32), 0.0).then_inc(zeroed, 1)
            nc.vector.memset(k_lo[0:HD, 1, :].bitcast(F32), 0.0).then_inc(zeroed, 1)
            for n, w in enumerate("vkq"):
                if w == "v":
                    for c in range(C):
                        dve.wait_ge(source_hi_ready, c + 1)
                        nc.vector.tensor_tensor(source_lo[0][:, c, :], source_raw[:, c, :], source_hi[0][:, c, :].bitcast(F32),
                                                ALU.subtract).then_inc(source_ready, 1)
                for c in range(C):
                    dve.wait_ge(weight_hi, C * n + c + 1)
                    nc.vector.tensor_tensor(wl[w][:, c, :], weight_raw[w][:, c, :], wh[w][:, c, :].bitcast(F32),
                                            ALU.subtract).then_inc(weight_lo, 1)
            dve.wait_ge(constants_in, 3 * 16)
            dve.wait_ge(zeroed, 6)

            def value_rest(g, parity, b):
                dve.wait_ge(proj_hi_ready, PROJ * g + b + 1)
                wait(dve, values_ready, GB * g + b - 1)
                nc.vector.tensor_tensor(v_rest[:, b % 2, :], proj_bank[b % 2][:], v_part[parity][0][:, b, :],
                                        ALU.subtract).then_inc(proj_split, 1)

            def key_low(g, u):
                dve.wait_ge(proj_hi_ready, PROJ * g + GB + 2 * u + 1)
                nc.vector.scalar_tensor_tensor(k_lo[0:HD, 0, :], proj_bank[0][0:HD, :], bias_k[0:HD, u:u + 1],
                                               k_hi[0:HD, 0, :].bitcast(F32), ALU.add, ALU.subtract)
                nc.vector.scalar_tensor_tensor(k_lo[HD:P, 1, :], proj_bank[0][HD:P, :], bias_k[HD:P, u:u + 1],
                                               k_hi[HD:P, 1, :].bitcast(F32), ALU.add, ALU.subtract).then_inc(proj_split, 1)

            def query_low(g, u):
                dve.wait_ge(proj_hi_ready, PROJ * g + GB + 2 * u + 2)
                nc.vector.scalar_tensor_tensor(q_lo[:], proj_bank[1][:], bias_q[:, u:u + 1], q_hi[:].bitcast(F32),
                                               ALU.add, ALU.subtract).then_inc(proj_split, 1)

            def mask_and_maximum(g, u):
                if u == 0:
                    dve.wait_ge(mask_ready, g + 1)
                for h in range(2):
                    gate(dve, scored, 2 * (C * g + u) + h + 1, dve_scratch[:, h:h + 1])
                    for j in range(4):
                        nc.vector.tensor_tensor_reduce(
                            out=probs[:, 4 * h + j, :], in0=score_bank[h][:, j * P:(j + 1) * P],
                            in1=mask[:, 2 * h + j // 2, :], scale=-SCALE, scalar=LARGEST, op0=ALU.add, op1=ALU.min,
                            accum_out=minus_max[:, 4 * h + j:4 * h + j + 1]).then_inc(masked, 1)

            def transposed_low(g, u, h):
                dve.wait_ge(pt_hi_ready, 2 * (C * g + u) + h + 1)
                nc.vector.tensor_tensor(pt_lo[:, 4 * h:4 * h + 4, :], pt_bank[h][:].rearrange("p (j i) -> p j i", j=4),
                                        pt_hi[:, 4 * h:4 * h + 4, :], ALU.subtract).then_inc(pt_split, 1)

            def divide(g, u):
                dve.wait_ge(exped, UNIT * (C * g + u + 1))
                nc.vector.reciprocal(row_inverse[:, u % 2, :], row_sum[:, u % 2, :]).then_inc(inverted, 1)
                dve.wait_ge(inverted, C * g + u + 1)
                dve.wait_ge(weighed, C * g + u + 1)
                nc.vector.tensor_tensor(
                    attended[:, :, u * P:(u + 1) * P].rearrange("p b (h d) -> p b h d", h=2),
                    out_bank[:].rearrange("p (b h d) -> p b h d", b=GB, h=2),
                    row_inverse[:, u % 2, :].rearrange("p (b h o) -> p b h o", b=GB, o=1).to_broadcast([P, GB, 2, HD]),
                    ALU.mult).then_inc(attended_ready, 1)

            def sum_and_stats(g, b):
                if b == 0:
                    dve.wait_ge(attended_ready, C * g + C)
                    if out_tokens is not None:
                        wait(dve, tokens_out, 16 * g)
                dve.wait_ge(biased, GB * g + b + 1)
                wait(dve, turned_ready, GB * g)
                nc.vector.tensor_tensor(normed[:, b, :], attended[:, b, :], tokens[:, b, :], ALU.add).then_inc(summed, 1)
                dve.wait_ge(summed, GB * g + b + 1)
                nc.vector.bn_stats(stats[:, b, :], normed[:, b, :]).then_inc(stats_ready, 1)
                gate(dve, stats_ready, GB * g + b + 1, dve_scratch[:, 2 + b:3 + b])
                nc.vector.bn_aggr(moments[:, b, :], stats[:, b, :]).then_inc(moments_ready, 1)

            def centre(g):
                dve.wait_ge(rstd_ready, g + 1)
                for b in range(GB):
                    nc.vector.tensor_scalar(normed[:, b, :], normed[:, b, :], moments[:, b, 0:1], rstd[:, b:b + 1],
                                            ALU.subtract, ALU.mult).then_inc(centred, 1)

            def body(g, parity):
                for u in range(C):
                    if u == 0:
                        if not ends(g):
                            dve.wait_ge(adj_in, 16 * g + 16)
                            wait(dve, masked, UNIT * C * g)
                            nc.vector.tensor_scalar(mask[:], adj[:], 0.0, MASKED, ALU.is_le, ALU.mult).then_inc(mask_ready, 1)
                            value_rest(g, parity, 0)
                        if not starts(g):
                            transposed_low(g - 1, C - 1, 0)
                        if not ends(g):
                            value_rest(g, parity, 1)
                        if not starts(g):
                            transposed_low(g - 1, C - 1, 1)
                        if not ends(g):
                            value_rest(g, parity, 2)
                        if not starts(g):
                            divide(g - 1, C - 1)
                            sum_and_stats(g - 1, 0)
                        if not ends(g):
                            value_rest(g, parity, 3)
                        if not starts(g):
                            sum_and_stats(g - 1, 1)
                        if not ends(g):
                            key_low(g, 0)
                        if not starts(g):
                            sum_and_stats(g - 1, 2)
                        if not ends(g):
                            query_low(g, 0)
                            mask_and_maximum(g, 0)
                        if not starts(g):
                            sum_and_stats(g - 1, 3)
                        continue
                    if not ends(g):
                        transposed_low(g, u - 1, 0)
                        key_low(g, u)
                        query_low(g, u)
                        transposed_low(g, u - 1, 1)
                        mask_and_maximum(g, u)
                        divide(g, u - 1)
                    if u == 1 and not starts(g):
                        centre(g - 1)

            over_groups(dve, body)

        @block.tensor
        def _(pe):
            def parts(a, b):
                return ((a[0], b[0]), (a[0], b[1]), (a[1], b[0]))

            def project(g, n, products, chunks=range(C)):
                if chunks[0] == 0:
                    wait(pe, proj_split, PROJ * g + n - 1)
                for c in chunks:
                    for i, (stationary, moving) in enumerate(products(c)):
                        last = nc.tensor.matmul(proj_bank[n % 2][:], stationary, moving, start=(c == 0 and i == 0),
                                                stop=(c == C - 1 and i == 2))
                if chunks[-1] == C - 1:
                    last.then_inc(projected, 1)

            def values(g, parity, b):
                if b == 0:
                    pe.wait_ge(source_ready, C * g + C)
                    if starts(g):
                        pe.wait_ge(weight_lo, C)
                x = [s[parity] for s in (source_hi, source_lo)]
                project(g, b, lambda c: parts([s[:, c, b * P:(b + 1) * P] for s in x],
                                              [w[:, c, :] for w in (wh["v"], wl["v"])]))

            def keys(g, parity, u, chunks=range(C)):
                if starts(g) and u == 0:
                    pe.wait_ge(weight_lo, 2 * C)
                x = [s[parity] for s in (source_hi, source_lo)]
                project(g, GB + 2 * u, lambda c: parts([w[:, c, u * P:(u + 1) * P] for w in (wh["k"], wl["k"])],
                                                       [s[:, c, :] for s in x]), chunks)

            def queries(g, parity, u):
                if u == 0:
                    if own_queries:
                        pe.wait_ge(query_ready, C * g + C)
                    if starts(g):
                        pe.wait_ge(weight_lo, 3 * C)
                x = (query_hi, query_lo) if own_queries else [s[parity] for s in (source_hi, source_lo)]
                project(g, GB + 2 * u + 1, lambda c: parts([w[:, c, u * P:(u + 1) * P] for w in (wh["q"], wl["q"])],
                                                           [s[:, c, :] for s in x]))

            def scores(g, u):
                if starts(g) and u == 0:
                    pe.wait_ge(zeroed, 6)
                    pe.wait_ge(constants_in, 3 * 16)
                pe.wait_ge(proj_split, PROJ * g + GB + 2 * u + 2)
                for h in range(2):
                    for i in range(2):
                        b = 2 * h + i
                        products = parts([q[:, b * P:(b + 1) * P] for q in (q_hi, q_lo)],
                                         [k[:, :, b * P:(b + 1) * P] for k in (k_hi, k_lo)])
                        for n, (q, k) in enumerate(products):
                            last = nc.tensor.matmul(
                                score_bank[h][:, 2 * i * P:2 * (i + 1) * P].rearrange("p (s j) -> p s j", s=2), q, k,
                                start=(n == 0), stop=(n == 2))
                    last.then_inc(scored, 1)

            def transposes(g, u, h):
                pe.wait_ge(exped, UNIT * (C * g + u) + 4 * (h + 1))
                for j in range(4):
                    last = nc.tensor.transpose(pt_bank[h][:, j * P:(j + 1) * P], probs[:, 4 * h + j, :], identity[:])
                last.then_inc(pt_ready, 1)

            def weigh(g, parity, u, h):
                if u == 0 and h == 0:
                    pe.wait_ge(values_ready, GB * g + GB)
                if h == 0:
                    wait(pe, attended_ready, C * g + u)
                pe.wait_ge(pt_split, 2 * (C * g + u) + h + 1)
                for j in range(4):
                    b, column = 2 * h + j // 2, u * P + (j % 2) * HD
                    v = [part[:, b, column:column + HD] for part in v_part[parity]]
                    hi, lo = pt_hi[:, 4 * h + j, :], pt_lo[:, 4 * h + j, :]
                    out = out_bank[:, (4 * h + j) * HD:(4 * h + j + 1) * HD]
                    products = ((hi, v[0]), (hi, v[1]), (hi, v[2]), (lo, v[0]), (lo, v[1]))
                    for n, (p, value) in enumerate(products):
                        last = nc.tensor.matmul(out, p, value, start=(n == 0), stop=(n == len(products) - 1))
                if h == 1:
                    last.then_inc(weighed, 1)

            def turn(g, b):
                pe.wait_ge(shifted, GB * g + b + 1)
                wait(pe, turned_copied, GB * g + b)
                for c in range(C):
                    last = nc.tensor.transpose(turn_bank[:, c * P:(c + 1) * P], normed[:, b, c * P:(c + 1) * P], identity[:])
                last.then_inc(turned_ready, 1)

            def body(g, parity):
                if not ends(g):
                    values(g, parity, 0)
                if not starts(g):
                    transposes(g - 1, C - 1, 0)
                if not ends(g):
                    values(g, parity, 1)
                if not starts(g):
                    transposes(g - 1, C - 1, 1)
                if not ends(g):
                    values(g, parity, 2)
                if not starts(g):
                    weigh(g - 1, 1 - parity, C - 1, 0)
                    weigh(g - 1, 1 - parity, C - 1, 1)
                if not ends(g):
                    values(g, parity, 3)
                    keys(g, parity, 0)
                    queries(g, parity, 0)
                for u in range(C):
                    turning = u == C - 1 and not starts(g)
                    if u > 0 and not ends(g):
                        keys(g, parity, u, range(1, C))
                        transposes(g, u - 1, 0)
                        queries(g, parity, u)
                    if turning:
                        turn(g - 1, 1)
                    if u > 0 and not ends(g):
                        transposes(g, u - 1, 1)
                        weigh(g, parity, u - 1, 0)
                    if turning:
                        turn(g - 1, 2)
                    if not ends(g):
                        if u < C - 1:
                            keys(g, parity, u + 1, range(1))
                        scores(g, u)
                        if u > 0:
                            weigh(g, parity, u - 1, 1)
                    if turning:
                        turn(g - 1, 3)
                    if u == C - 2 and not starts(g):
                        turn(g - 1, 0)

            over_groups(pe, body)


def feed_forward_pass(nc, source, nodes, x, w1, b1, w2, b2, gain, shift, out):
    name = "ffn"
    with ExitStack() as ctx:
        def sb(n, shape, dtype=F32):
            return ctx.enter_context(nc.sbuf_tensor(f"{name}_{n}", shape, dtype))

        def sem(n):
            return ctx.enter_context(nc.semaphore(f"{name}_{n}"))

        def bank(n):
            return ctx.enter_context(nc.psum_tensor(f"{name}_{n}", [P, 512], F32))

        w1_hi, w1_lo = (sb(f"w1_{s}", [P, C, FF], F32R) for s in ("hi", "lo"))
        w2_hi, w2_lo = (sb(f"w2_{s}", [P, FC, D], F32R) for s in ("hi", "lo"))
        bias_1 = sb("bias_1", [P, FC])
        bias_2 = sb("bias_2", [P, D])
        gain_row = sb("gain_row", [P, D])
        shift_row = sb("shift_row", [P, D])
        half = sb("minus_half", [P, GB])
        dve_scratch = sb("dve_scratch", [P, 2 + GB])
        pool_scratch = sb("pool_scratch", [P, 4])
        source_raw = sb("source_raw", [P, C, GT])
        source_hi = [sb(f"source_hi{p}", [P, C, GT], F32R) for p in range(2)]
        source_lo = [sb(f"source_lo{p}", [P, C, GT], F32R) for p in range(2)]
        hidden = sb("hidden", [P, 2, GT])
        hidden_hi = sb("hidden_hi", [P, 2, GT], F32R)
        hidden_lo = sb("hidden_lo", [P, 2, GT], F32R)
        tokens = sb("tokens", [P, GB, D])
        x_tile = sb("x_tile", [P, 2, D])
        stats = sb("stats", [P, GB, 6])
        moments = sb("moments", [P, GB, 2])
        spread = sb("spread", [P, GB])
        rstd = sb("rstd", [P, GB])

        up_bank = [bank(f"up{i}") for i in range(2)]
        down_bank = [bank(f"down{i}") for i in range(GB)]

        weights_in = [sem(f"weights_in{i}") for i in range(2)]
        constants_in, source_in, tokens_in = sem("constants_in"), sem("source_in"), sem("tokens_in")
        x_in = [sem("x_in0"), sem("x_in1")]
        zeroed, weight_hi, weight_lo = sem("zeroed"), sem("weight_hi"), sem("weight_lo")
        source_hi_ready, source_ready = sem("source_hi_ready"), sem("source_ready")
        raised, activated, hidden_hi_ready, hidden_ready = sem("raised"), sem("activated"), sem("hidden_hi_ready"), sem("hidden_ready")
        lowered, biased, summed = sem("lowered"), sem("biased"), sem("summed")
        stats_ready, moments_ready = sem("stats_ready"), sem("moments_ready")
        spread_ready, rstd_ready, centred = sem("spread_ready"), sem("rstd_ready"), sem("centred")
        gained, shifted, topped = sem("gained"), sem("shifted"), sem("topped")
        stored = sem("stored")

        source_view = source.rearrange("(c p) t -> p c t", p=P)
        nodes_view = nodes.rearrange("(b p) d -> p b d", p=P)
        x_view = x.rearrange("(b p) d -> p b d", p=P)
        out_view = out.rearrange("(b p) d -> p b d", p=P)
        w1_view = w1.rearrange("(c p) n -> p c n", p=P)
        w2_view = w2.rearrange("(c p) n -> p c n", p=P)
        pieces = []
        for n in range(FC // 4):
            for k in range(0, C, 2):
                pieces.append([w[:, k:k + 2, n * D:(n + 1) * D] for w in (w1_view, w1_hi, w1_lo)])
            for k in range(4 * n, 4 * n + 4, 2):
                pieces.append([w[:, k:k + 2, :] for w in (w2_view, w2_hi, w2_lo)])
        AHEAD = 4
        weight_raw = [tokens[:, 0:2, :], tokens[:, 2:4, :]]

        block = ctx.enter_context(nc.Block())

        @block.sync
        def _(sp):
            sp.dma_start(source_raw[:], source_view[:, :, 0:GT]).then_inc(source_in, 16)
            for n, (matrix, _, _) in enumerate(pieces):
                wait(sp, weight_lo, n - 1)
                sp.dma_start(weight_raw[n % 2], matrix).then_inc(weights_in[n % 2], 16)
                if n == 1:
                    for tile, data in ((bias_1[:], b1), (bias_2[:], row(b2)), (gain_row[:], row(gain)), (shift_row[:], row(shift))):
                        sp.dma_start(tile, data).then_inc(constants_in, 16)
                if n == 4:
                    sp.wait_ge(source_ready, C)
                    sp.dma_start(source_raw[:], source_view[:, :, GT:2 * GT]).then_inc(source_in, 16)
            sp.wait_ge(weight_lo, len(pieces))

            def body(g, parity):
                if whole(g) and not starts(g):
                    wait(sp, source_ready, C * g + C)
                    sp.dma_start(source_raw[:], source_view[:, :, bass.ds((g + 1) * GT, GT)]).then_inc(source_in, 16)
                if not starts(g):
                    for b in range(GB):
                        n = GB * (g - 1) + b
                        if b >= 2:
                            sp.wait_ge(topped, GB * (g - 1) + b - 1)
                        sp.dma_start(x_tile[:, b % 2, :], x_view[:, (g - 1) * GB + b, :] if isinstance(g, int)
                                     else x_view[:, bass.ds((g - 1) * GB + b, 1), :].rearrange("p b d -> p (b d)")).then_inc(x_in[b % 2], 16)
                    wait(sp, centred, 2 * GB * g)
                    sp.dma_start(out_view[:, bass.ds((g - 1) * GB, GB), :], tokens[:]).then_inc(stored, 16)
                if not ends(g):
                    wait(sp, stored, 16 * g)
                    sp.dma_start(tokens[:], nodes_view[:, bass.ds(g * GB, GB), :]).then_inc(tokens_in, 16)

            over_groups(sp, body)
            sp.wait_ge(stored, 16 * NG)

        @block.scalar
        def _(act):
            def weight_high(n):
                act.wait_ge(weights_in[n % 2], 16 * (n // 2 + 1))
                nc.scalar.copy(pieces[n][1], weight_raw[n % 2]).then_inc(weight_hi, 1)

            act.wait_ge(source_in, 16)
            for c in range(C):
                nc.scalar.copy(source_hi[0][:, c, :], source_raw[:, c, :]).then_inc(source_hi_ready, 1)
            for n in range(AHEAD):
                weight_high(n)
            act.wait_ge(constants_in, 4 * 16)

            def hidden_high(g, c):
                act.wait_ge(activated, FC * g + c + 1)
                nc.scalar.copy(hidden_hi[:, c % 2, :], hidden[:, c % 2, :]).then_inc(hidden_hi_ready, 1)

            def body(g, parity):
                for c in range(FC):
                    if not ends(g):
                        act.wait_ge(raised, FC * g + c + 1)
                        wait(act, hidden_ready, FC * g + c - 1)
                        nc.scalar.activation(hidden[:, c % 2, :], up_bank[c % 2][:], ACT.Gelu,
                                             bias=bias_1[:, c:c + 1]).then_inc(activated, 1)
                        hidden_high(g, c)
                        if starts(g) and AHEAD + c < len(pieces):
                            weight_high(AHEAD + c)
                    if 8 <= c < 8 + C and whole(g):
                        if c == 8:
                            act.wait_ge(source_in, 16 * g + 32)
                        nc.scalar.copy(source_hi[1 - parity][:, c - 8, :], source_raw[:, c - 8, :]).then_inc(source_hi_ready, 1)

            over_groups(act, body)

        @block.gpsimd
        def _(pool):
            nc.gpsimd.memset(half[:], -0.5).then_inc(zeroed, 1)
            nc.gpsimd.memset(pool_scratch[:], 0.0).then_inc(zeroed, 1)
            pool.wait_ge(zeroed, 2)
            pool.wait_ge(constants_in, 4 * 16)

            def inverse_spread(g, norm):
                n = 2 * g + norm
                pool_gate(pool, moments_ready, GB * (n + 1), pool_scratch)
                nc.gpsimd.tensor_scalar(spread[:], moments[:, :, 1], EPS, None, ALU.add).then_inc(spread_ready, 1)
                pool.wait_ge(spread_ready, n + 1)
                nc.gpsimd.tensor_tensor(rstd[:], spread[:], half[:], ALU.pow).then_inc(rstd_ready, 1)

            def body(g, parity):
                if not starts(g):
                    inverse_spread(g - 1, 0)
                    for b in range(GB):
                        n = GB * (g - 1) + b + 1
                        pool.wait_ge(centred, 2 * GB * (g - 1) + b + 1)
                        nc.gpsimd.tensor_tensor(tokens[:, b, :], tokens[:, b, :], gain_row[:], ALU.mult).then_inc(gained, 1)
                        pool.wait_ge(gained, n)
                        nc.gpsimd.tensor_tensor(tokens[:, b, :], tokens[:, b, :], shift_row[:], ALU.add).then_inc(shifted, 1)
                        pool.wait_ge(shifted, n)
                        pool.wait_ge(x_in[b % 2], 16 * (2 * (g - 1) + b // 2 + 1))
                        nc.gpsimd.tensor_tensor(tokens[:, b, :], tokens[:, b, :], x_tile[:, b % 2, :], ALU.add).then_inc(topped, 1)
                    inverse_spread(g - 1, 1)
                if whole(g):
                    for c in range(C):
                        pool.wait_ge(source_hi_ready, C * g + C + c + 1)
                        nc.gpsimd.tensor_tensor(source_lo[1 - parity][:, c, :], source_raw[:, c, :],
                                                source_hi[1 - parity][:, c, :].bitcast(F32), ALU.subtract).then_inc(source_ready, 1)
                if not ends(g):
                    pool.wait_ge(tokens_in, 16 * g + 16)
                    for b in range(GB):
                        nc.gpsimd.tensor_tensor(tokens[:, b, :], tokens[:, b, :], bias_2[:], ALU.add).then_inc(biased, 1)

            over_groups(pool, body)

        @block.vector
        def _(dve):
            def weight_low(n):
                _, hi, lo = pieces[n]
                dve.wait_ge(weight_hi, n + 1)
                nc.vector.tensor_tensor(lo, weight_raw[n % 2], hi.bitcast(F32), ALU.subtract).then_inc(weight_lo, 1)

            for c in range(C):
                dve.wait_ge(source_hi_ready, c + 1)
                nc.vector.tensor_tensor(source_lo[0][:, c, :], source_raw[:, c, :], source_hi[0][:, c, :].bitcast(F32),
                                        ALU.subtract).then_inc(source_ready, 1)
            for n in range(AHEAD):
                weight_low(n)

            def moments_of(g, norm, b):
                n = 2 * GB * g + GB * norm + b + 1
                nc.vector.bn_stats(stats[:, b, :], tokens[:, b, :]).then_inc(stats_ready, 1)
                gate(dve, stats_ready, n, dve_scratch[:, b:b + 1])
                nc.vector.bn_aggr(moments[:, b, :], stats[:, b, :]).then_inc(moments_ready, 1)

            def centre(g, norm):
                dve.wait_ge(rstd_ready, 2 * g + norm + 1)
                for b in range(GB):
                    nc.vector.tensor_scalar(tokens[:, b, :], tokens[:, b, :], moments[:, b, 0:1], rstd[:, b:b + 1],
                                            ALU.subtract, ALU.mult).then_inc(centred, 1)

            def body(g, parity):
                for c in range(FC):
                    if not ends(g):
                        dve.wait_ge(hidden_hi_ready, FC * g + c + 1)
                        nc.vector.tensor_tensor(hidden_lo[:, c % 2, :], hidden[:, c % 2, :], hidden_hi[:, c % 2, :].bitcast(F32),
                                                ALU.subtract).then_inc(hidden_ready, 1)
                    if starts(g):
                        if AHEAD + c < len(pieces):
                            weight_low(AHEAD + c)
                        continue
                    if c == 0:
                        for b in range(GB):
                            dve.wait_ge(lowered, GB * (g - 1) + b + 1)
                            dve.wait_ge(biased, GB * (g - 1) + b + 1)
                            nc.vector.tensor_tensor(tokens[:, b, :], down_bank[b][:], tokens[:, b, :], ALU.add).then_inc(summed, 1)
                    if 2 <= c < 2 + GB:
                        b = c - 2
                        dve.wait_ge(summed, GB * (g - 1) + b + 1)
                        moments_of(g - 1, 0, b)
                    if c == 7:
                        centre(g - 1, 0)
                    if c == 11:
                        for b in range(GB):
                            dve.wait_ge(topped, GB * (g - 1) + b + 1)
                            moments_of(g - 1, 1, b)
                    if c == 13:
                        centre(g - 1, 1)

            over_groups(dve, body)

        @block.tensor
        def _(pe):
            def parts(a, b):
                return ((a[0], b[0]), (a[0], b[1]), (a[1], b[0]))

            def up(g, parity, c):
                if c == 0:
                    pe.wait_ge(source_ready, C * g + C)
                if starts(g) and c % 4 == 0:
                    pe.wait_ge(weight_lo, c + 2)
                wait(pe, activated, FC * g + c - 1)
                products = [p for k in range(C)
                            for p in parts([w[:, k, c * P:(c + 1) * P] for w in (w1_hi, w1_lo)],
                                           [s[parity][:, k, :] for s in (source_hi, source_lo)])]
                for i, (w, s) in enumerate(products):
                    last = nc.tensor.matmul(up_bank[c % 2][:], w, s, start=(i == 0), stop=(i == len(products) - 1))
                last.then_inc(raised, 1)

            def down(g, c):
                if starts(g) and c % 4 == 0:
                    pe.wait_ge(weight_lo, c + 4)
                pe.wait_ge(hidden_ready, FC * g + c + 1)
                if c == 0:
                    wait(pe, summed, GB * g)
                for b in range(GB):
                    products = parts([h[:, c % 2, b * P:(b + 1) * P] for h in (hidden_hi, hidden_lo)],
                                     [w[:, c, :] for w in (w2_hi, w2_lo)])
                    for i, (h, w) in enumerate(products):
                        last = nc.tensor.matmul(down_bank[b][:], h, w, start=(c == 0 and i == 0), stop=(c == FC - 1 and i == 2))
                    if c == FC - 1:
                        last.then_inc(lowered, 1)

            def body(g, parity):
                for c in range(FC):
                    if not ends(g):
                        up(g, parity, c)
                    if c > 0 and not ends(g):
                        down(g, c - 1)
                    if c == 0 and not starts(g):
                        down(g - 1, FC - 1)

            over_groups(pe, body)


def build(nc, xt, x, adj_t, adj, ident, n2e, e2n, ffn, scratch, out):
    attention_pass(nc, "n2e", None, xt, x, adj_t, *n2e, ident, scratch["edges_t"], None)
    attention_pass(nc, "e2n", xt, scratch["edges_t"], x, adj, *e2n, ident, scratch["nodes_t"], scratch["nodes"])
    feed_forward_pass(nc, scratch["nodes_t"], scratch["nodes"], x, *ffn, out)


def kernel(**inputs):
    import numpy as np
    import concourse.bacc as bacc
    from concourse.bass_utils import run_bass_kernel_spmd

    def weights_t(name):
        return np.ascontiguousarray(np.asarray(inputs["L0_gnn_" + name]).T)

    def vector(name):
        return np.ascontiguousarray(inputs["L0_gnn_" + name])

    def columns(name):
        return np.ascontiguousarray(vector(name).reshape(-1, P).T)

    x = np.ascontiguousarray(inputs["x"]).reshape(T, D)
    adj = np.asarray(inputs["adj"])
    arrays = {
        "x": x,
        "x_t": np.ascontiguousarray(x.T),
        "adj_nodes": np.ascontiguousarray(adj.transpose(1, 0, 2)),
        "adj_edges": np.ascontiguousarray(adj.transpose(2, 0, 1)),
        "identity": np.eye(P, dtype=np.float32),
    }
    for side, norm in (("n2e", "norm1"), ("e2n", "norm2")):
        for p in "qkv":
            arrays[f"{side}_{p}_w"] = weights_t(f"{side}_{p}_w")
        for p in "qk":
            arrays[f"{side}_{p}_b"] = columns(f"{side}_{p}_b")
        arrays[f"{side}_v_b"] = vector(f"{side}_v_b")
        for p in "gb":
            arrays[f"{side}_norm_{p}"] = vector(f"{norm}_{p}")
    arrays |= {"w1": weights_t("ffn_w1"), "b1": columns("ffn_b1"), "w2": weights_t("ffn_w2"), "b2": vector("ffn_b2"),
               "norm_g": vector("norm3_g"), "norm_b": vector("norm3_b")}

    nc = bacc.Bacc("TRN2", target_bir_lowering=False, num_devices=1)
    a = {}
    for name, array in arrays.items():
        a[name] = nc.dram_tensor(f"in_{name}", array.shape, mybir.dt.from_np(array.dtype), kind="ExternalInput").ap()
    out = nc.dram_tensor("out", (T, D), F32, kind="ExternalOutput").ap()
    scratch = {"edges_t": nc.dram_tensor("edges_t", (D, T), F32).ap(),
               "nodes_t": nc.dram_tensor("nodes_t", (D, T), F32).ap(),
               "nodes": nc.dram_tensor("nodes", (T, D), F32).ap()}

    def side(s):
        return tuple(a[f"{s}_{n}"] for n in ("q_w", "k_w", "v_w", "q_b", "k_b", "v_b", "norm_g", "norm_b"))

    build(nc, a["x_t"], a["x"], a["adj_edges"], a["adj_nodes"], a["identity"], side("n2e"), side("e2n"),
          (a["w1"], a["b1"], a["w2"], a["b2"], a["norm_g"], a["norm_b"]), scratch, out)
    result = run_bass_kernel_spmd(nc, [{f"in_{n}": v for n, v in arrays.items()}], core_ids=[0])
    return result.results[0]["out"].reshape(B, P, D)
```

```python
from contextlib import ExitStack

import concourse.bass as bass
from concourse import mybir

P = 128
D = 512
C = D // P
B = 64
T = B * P
GB = 4
GT = GB * P
NG = B // GB
H = 8
HD = D // H
FF = 4 * D
FC = FF // P
SCALE = float(HD) ** -0.5
EPS = 1e-5
MASKED = -1e30
LARGEST = 3e38

F32 = mybir.dt.float32
F32R = mybir.dt.float32r
F16 = mybir.dt.float16
BF16 = mybir.dt.bfloat16
ALU = mybir.AluOpType
ACT = mybir.ActivationFunctionType

PROJ = GB + 2 * C
VALUE_PLACE = (0, 1, 2, 5)
KEY_PLACE = (3, 6, 8, 10)
QUERY_PLACE = (4, 7, 9, 11)
UNIT = GB * 2

NORM_TILES = {"dve_scratch": [P, 2 + GB], "stats": [P, GB, 6], "moments": [P, GB, 2],
              "spread": [P, GB], "rstd": [P, GB]}


def wait(engine, semaphore, value):
    if isinstance(value, int) and value <= 0:
        return
    engine.wait_ge(semaphore, value)


def gate(engine, semaphore, value, scratch):
    if not isinstance(value, int):
        engine.wait_ge(semaphore, value)
        engine.memset(scratch, 0.0)
    else:
        engine.wait_ge(semaphore, value)


def pool_gate(engine, semaphore, value, scratch):
    engine.wait_ge(semaphore, value)
    if not isinstance(value, int):
        engine.tensor_tensor(scratch[:, 0:1], scratch[:, 1:2], scratch[:, 2:3], ALU.add)


def over_groups(engine, body, start=0):
    body(start, 0)
    body(start + 1, 1)
    with engine.Fori(start // 2 + 1, (start + NG) // 2 - 1) as i:
        body(2 * i, 0)
        body(2 * i + 1, 1)
    body(start + NG - 2, 0)
    body(start + NG - 1, 1)


def row(vector):
    return vector.rearrange("(a d) -> a d", a=1).to_broadcast([P, D])


class Shared:

    def __init__(self, nc, ctx):
        def sb(n, shape, dtype=F32):
            return ctx.enter_context(nc.sbuf_tensor(n, shape, dtype))

        def sem(n):
            return ctx.enter_context(nc.semaphore(n))

        self.weight_hi = {w: sb(f"weight_{w}_hi", [P, C, D], F32R) for w in "vkq"}
        self.weight_lo = {w: sb(f"weight_{w}_lo", [P, C, D], F32R) for w in "vkq"}
        self.source_raw = sb("source_raw", [P, C, GT])
        self.source_hi = [sb(f"source_hi{p}", [P, C, GT], F32R) for p in range(2)]
        self.source_lo = [sb(f"source_lo{p}", [P, C, GT], F32R) for p in range(2)]
        self.bias_row = sb("bias_row", [P, D])
        self.gain_row = sb("gain_row", [P, D])
        self.shift_row = sb("shift_row", [P, D])
        self.normed = sb("normed", [P, GB, D])
        self.turned = sb("turned", [P, 2, C, P])
        self.half = sb("minus_half", [P, GB])
        self.pool_scratch = sb("pool_scratch", [P, 4])
        self.attention = {n: sb(f"att_{n}", shape) for n, shape in {
            "identity": [P, P], "bias_q0": [P, C], "bias_q1": [P, C], "bias_k0": [P, C], "bias_k1": [P, C],
            "minus_max": [P, UNIT], "row_sum": [P, 2, UNIT], "row_inverse": [P, 2, UNIT], **NORM_TILES}.items()}
        self.feed_forward = {n: sb(f"ffn_{n}", shape) for n, shape in {"bias_1": [P, FC], **NORM_TILES}.items()}
        self.proj_bank, self.score_bank, self.pt_bank = (
            [ctx.enter_context(nc.psum_tensor(f"{n}{i}", [P, 512], F32)) for i in range(2)] for n in ("proj", "score", "pt"))
        self.source_in, self.source_hi_ready, self.source_ready = sem("source_in"), sem("source_hi_ready"), sem("source_ready")
        self.bias_row_in, self.norm_in = sem("bias_row_in"), sem("norm_in")
        self.turned_out = [sem("turned_out0"), sem("turned_out1")]


class FeedForwardWeights:

    def __init__(self, nc, ctx, m, w1, w2):
        with ExitStack() as reused:
            def sb(n, shape, dtype=F32R):
                return reused.enter_context(nc.sbuf_tensor(n, shape, dtype))

            def block_of(n):
                return sb(f"{n}_hi", [P, C, D]), sb(f"{n}_lo", [P, C, D])

            self.raw = sb("ffn_weight_raw", [P, C, D], F32)
            second_2 = block_of("w2_1")
            self.hidden = sb("hidden", [P, 2, GT], F32)
            self.hidden_hi = sb("hidden_hi", [P, 2, GT])
            self.hidden_lo = sb("hidden_lo", [P, 2, GT])
            others = [block_of(n) for n in ("w1_2", "w2_2", "w1_3", "w2_3")]
        first, second, third = ((m.weight_hi[w], m.weight_lo[w]) for w in "vkq")
        self.w1 = [first, third, others[0], others[2]]
        self.w2 = [second, second_2, others[1], others[3]]
        w1_view = w1.rearrange("(c p) n -> p c n", p=P)
        w2_view = w2.rearrange("(c p) n -> p c n", p=P)
        self.pieces = []
        for n in range(FC // 4):
            for k in range(0, C, 2):
                self.pieces.append((w1_view[:, k:k + 2, n * D:(n + 1) * D], *(w[:, k:k + 2, :] for w in self.w1[n])))
            for k in range(0, 4, 2):
                self.pieces.append((w2_view[:, 4 * n + k:4 * n + k + 2, :], *(w[:, k:k + 2, :] for w in self.w2[n])))
        self.arrived = [ctx.enter_context(nc.semaphore(f"ffn_weights_in{i}")) for i in range(2)]
        self.hi_ready, self.ready = (ctx.enter_context(nc.semaphore(f"ffn_weight_{n}")) for n in ("hi_ready", "ready"))
        self.nc = nc

    def load(self, sp, n):
        wait(sp, self.ready, n - 1)
        half = self.raw[:, 2 * (n % 2):2 * (n % 2) + 2, :]
        sp.dma_start(half, self.pieces[n][0]).then_inc(self.arrived[n % 2], 16)

    def high(self, act, n):
        act.wait_ge(self.arrived[n % 2], 16 * (n // 2 + 1))
        half = self.raw[:, 2 * (n % 2):2 * (n % 2) + 2, :]
        self.nc.scalar.copy(self.pieces[n][1], half).then_inc(self.hi_ready, 1)

    def low(self, dve, n):
        _, hi, lo = self.pieces[n]
        dve.wait_ge(self.hi_ready, n + 1)
        half = self.raw[:, 2 * (n % 2):2 * (n % 2) + 2, :]
        self.nc.vector.tensor_tensor(lo, half, hi.bitcast(F32), ALU.subtract).then_inc(self.ready, 1)


def attention_passes(nc, ctx, m, block, passes, feed_forward, nodes_features, residual, identity_in):
    last_group = 2 * NG
    AHEAD = ((0,), (1,), (2, 3), ())

    def starts(group):
        return isinstance(group, int) and group == 0

    def ends(group):
        return isinstance(group, int) and group == last_group

    def opens(group):
        return isinstance(group, int) and group % NG == 0 and group < last_group

    def over_passes(engine, body):
        for n in range(2):
            def neighbours(group, parity):
                if isinstance(group, int):
                    body(group, parity, (group - 1) // NG, n, (group + 1) // NG)
                else:
                    body(group, parity, n, n, n)

            over_groups(engine, neighbours, n * NG)
        body(last_group, 0, 1, None, None)

    def sb(n, shape, dtype, where):
        return where.enter_context(nc.sbuf_tensor(f"att_{n}", shape, dtype))

    def sem(n):
        return ctx.enter_context(nc.semaphore(f"att_{n}"))

    def bank(n):
        return ctx.enter_context(nc.psum_tensor(f"att_{n}", [P, 512], F32))

    wh, wl, source_raw, source_hi, source_lo = m.weight_hi, m.weight_lo, m.source_raw, m.source_hi, m.source_lo
    bias_v, gain_row, shift_row, normed, turned, half = m.bias_row, m.gain_row, m.shift_row, m.normed, m.turned, m.half
    proj_bank, score_bank, pt_bank = m.proj_bank, m.score_bank, m.pt_bank
    out_bank, turn_bank = bank("out"), bank("turn")
    small = m.attention
    identity, minus_max, row_sum, row_inverse = (small[n] for n in ("identity", "minus_max", "row_sum", "row_inverse"))
    bias_q, bias_k = ([small[f"bias_{w}{n}"] for n in range(2)] for w in "qk")
    pool_scratch = m.pool_scratch
    dve_scratch, stats, moments, spread, rstd = (small[n] for n in NORM_TILES)

    with ExitStack() as early:
        weight_raw = {w: sb(f"weight_{w}_raw", [P, C, D], F32, early) for w in "vkq"}
    with ExitStack() as reused:
        query_raw = sb("query_raw", [P, C, GT], F32, reused)
        query_hi = sb("query_hi", [P, C, GT], F32R, reused)
        query_lo = sb("query_lo", [P, C, GT], F32R, reused)
        q_hi = sb("q_hi", [P, GT], F32R, reused)
        q_lo = sb("q_lo", [P, GT], F32R, reused)
        k_hi = sb("k_hi", [P, 2, GT], F32R, reused)
        k_lo = sb("k_lo", [P, 2, GT], F32R, reused)
        v_part = [[sb(f"v{i}_{p}", [P, GB, D], BF16, reused) for i in range(3)] for p in range(2)]
        v_rest = sb("v_rest", [P, 2, D], F32, reused)
        adj = sb("adj", [P, GB, P], F32, reused)
        mask = sb("mask", [P, GB, P], F32, reused)
        probs = sb("probs", [P, UNIT, P], F32, reused)
        pt_hi = sb("pt_hi", [P, UNIT, P], F16, reused)
        pt_lo = sb("pt_lo", [P, UNIT, P], F16, reused)
        tokens = sb("tokens", [P, GB, D], F32, reused)
        attended = sb("attended", [P, GB, D], F32, reused)

    weights_in = {w: sem(f"weight_{w}_in") for w in "vkq"}
    constants_in, query_in, adj_in, tokens_in = sem("constants_in"), sem("query_in"), sem("adj_in"), sem("tokens_in")
    source_in, bias_v_in, norm_in = m.source_in, m.bias_row_in, m.norm_in
    weight_hi, weight_lo = sem("weight_hi"), sem("weight_lo")
    zeroed = sem("zeroed")
    source_hi_ready, source_ready = m.source_hi_ready, m.source_ready
    query_hi_ready, query_ready = sem("query_hi_ready"), sem("query_ready")
    key_half_ready = sem("key_half_ready")
    projected, proj_hi_ready, proj_split = sem("projected"), sem("proj_hi_ready"), sem("proj_split")
    v_middle_ready, values_ready = sem("v_middle_ready"), sem("values_ready")
    mask_ready = sem("mask_ready")
    scored, masked, exped = sem("scored"), sem("masked"), sem("exped")
    pt_ready, pt_hi_ready, pt_split = sem("pt_ready"), sem("pt_hi_ready"), sem("pt_split")
    weighed, inverted, attended_ready = sem("weighed"), sem("inverted"), sem("attended_ready")
    biased, summed, stats_ready, moments_ready = sem("biased"), sem("summed"), sem("stats_ready"), sem("moments_ready")
    spread_ready, rstd_ready, centred = sem("spread_ready"), sem("rstd_ready"), sem("centred")
    gained, shifted = sem("gained"), sem("shifted")
    turned_ready, turned_copied = sem("turned_ready"), sem("turned_copied")
    turned_out = m.turned_out
    tokens_out = sem("tokens_out")

    source_view = [f.rearrange("(c p) t -> p c t", p=P) for f in (passes[0]["source"], passes[1]["source"], nodes_features)]
    query_view = passes[1]["query_source"].rearrange("(c p) t -> p c t", p=P)
    residual_view = residual.rearrange("(b p) d -> p b d", p=P)
    out_view = [p["out_features"].rearrange("(c p) t -> p c t", p=P) for p in passes]
    out_tokens_view = passes[1]["out_tokens"].rearrange("(b p) d -> p b d", p=P)

    @block.sync
    def _(sp):
        def weight_in(n, w):
            sp.dma_start(weight_raw[w][:], passes[n]["w" + w].rearrange("(c p) n -> p c n", p=P)).then_inc(weights_in[w], 16)

        def value_bias_in(n):
            sp.dma_start(bias_v[:], row(passes[n]["bv"])).then_inc(bias_v_in, 16)

        def norm_rows_in(n):
            for tile, data in ((gain_row[:], row(passes[n]["gain"])), (shift_row[:], row(passes[n]["shift"]))):
                sp.dma_start(tile, data).then_inc(norm_in, 16)

        sp.dma_start(source_raw[:], source_view[0][:, :, 0:GT]).then_inc(source_in, 16)
        weight_in(0, "v")
        for tile, data in ((identity[:], identity_in), (bias_q[0][:], passes[0]["bq"]), (bias_k[0][:], passes[0]["bk"]),
                           (bias_q[1][:], passes[1]["bq"]), (bias_k[1][:], passes[1]["bk"])):
            sp.dma_start(tile, data).then_inc(constants_in, 16)
        sp.dma_start(adj[:], passes[0]["adjacency"][:, 0:GB, :]).then_inc(adj_in, 16)
        weight_in(0, "k")
        weight_in(0, "q")
        value_bias_in(0)
        norm_rows_in(0)

        def body(g, parity, before, own, after):
            if ends(g):
                return
            following = g + 1 - after * NG
            sp.wait_ge(source_ready, C * g + C)
            if after >= 1:
                for s in turned_out:
                    sp.wait_ge(s, 32 * ((after - 1) * NG + following + 1))
            sp.dma_start(source_raw[:], source_view[after][:, :, bass.ds(following * GT, GT)]).then_inc(source_in, 16)
            if after < 2:
                sp.wait_ge(mask_ready, g + 1)
                sp.dma_start(adj[:], passes[after]["adjacency"][:, bass.ds(following * GB, GB), :]).then_inc(adj_in, 16)
            wait(sp, summed, GB * g)
            sp.dma_start(tokens[:], residual_view[:, bass.ds((g - own * NG) * GB, GB), :]).then_inc(tokens_in, 16)
            if after == 1:
                if own == 0:
                    sp.wait_ge(weight_lo, 4 * C)
                else:
                    sp.wait_ge(query_ready, C * following)
                sp.dma_start(query_raw[:], query_view[:, :, bass.ds(following * GT, GT)]).then_inc(query_in, 16)
            if after == 2:
                sp.wait_ge(query_ready, C * NG)
                for n in range(4):
                    feed_forward.load(sp, n)
            if starts(g):
                sp.wait_ge(weight_lo, 3 * C)
                for w in "vkq":
                    weight_in(1, w)
            else:
                last = g - 1 - before * NG
                for b in range(GB):
                    sp.wait_ge(turned_copied, GB * (g - 1) + b + 1)
                    sp.dma_start(out_view[before][:, :, bass.ds(last * GT + b * P, P)], turned[:, b % 2]).then_inc(turned_out[b % 2], 16)
                if before == 1:
                    sp.wait_ge(shifted, GB * g)
                    sp.dma_start(out_tokens_view[:, bass.ds(last * GB, GB), :], normed[:]).then_inc(tokens_out, 16)
            if isinstance(g, int) and g == NG - 1:
                sp.wait_ge(biased, GB * NG)
                value_bias_in(1)
            if isinstance(g, int) and g == NG:
                sp.wait_ge(shifted, GB * NG)
                norm_rows_in(1)

        over_passes(sp, body)

    def store_last(sp, b):
        sp.wait_ge(turned_copied, GB * (last_group - 1) + b + 1)
        sp.dma_start(out_view[1][:, :, (NG - 1) * GT + b * P:(NG - 1) * GT + (b + 1) * P], turned[:, b % 2]).then_inc(turned_out[b % 2], 16)

    def store_last_tokens(sp):
        sp.wait_ge(shifted, GB * last_group)
        sp.dma_start(out_tokens_view[:, (NG - 1) * GB:NG * GB, :], normed[:]).then_inc(tokens_out, 16)
        sp.wait_ge(turned_ready, GB * last_group)
        sp.wait_ge(tokens_out, 16 * NG)

    def copy_turned(act, g, b):
        act.wait_ge(turned_ready, GB * g + b + 1)
        wait(act, turned_out[b % 2], 16 * (2 * g + b // 2))
        nc.scalar.copy(turned[:, b % 2], turn_bank[:].rearrange("p (c t) -> p c t", c=C)).then_inc(turned_copied, 1)

    @block.scalar
    def _(act):
        act.wait_ge(source_in, 16)
        for c in range(C):
            nc.scalar.copy(source_hi[0][:, c, :], source_raw[:, c, :]).then_inc(source_hi_ready, 1)

        def weights_high(n, w, chunks=range(C)):
            for c in chunks:
                if c == 0:
                    act.wait_ge(weights_in[w], 16 * n + 16)
                nc.scalar.copy(wh[w][:, c, :], weight_raw[w][:, c, :]).then_inc(weight_hi, 1)

        for w in "vk":
            weights_high(0, w)
        act.wait_ge(constants_in, 5 * 16)
        act.wait_ge(zeroed, 6)

        def value_high(g, parity, b):
            n = VALUE_PLACE[b]
            act.wait_ge(projected, PROJ * g + n + 1)
            nc.scalar.copy(v_part[parity][0][:, b, :], proj_bank[n % 2][:]).then_inc(proj_hi_ready, 1)

        def key_high(g, own, u):
            n = KEY_PLACE[u]
            act.wait_ge(projected, PROJ * g + n + 1)
            nc.scalar.activation(k_hi[0:HD, 0, :], proj_bank[n % 2][0:HD, :], ACT.Identity,
                                 bias=bias_k[own][0:HD, u:u + 1]).then_inc(key_half_ready, 1)
            nc.scalar.activation(k_hi[HD:P, 1, :], proj_bank[n % 2][HD:P, :], ACT.Identity,
                                 bias=bias_k[own][HD:P, u:u + 1]).then_inc(proj_hi_ready, 1)

        def query_high(g, own, u):
            n = QUERY_PLACE[u]
            act.wait_ge(projected, PROJ * g + n + 1)
            nc.scalar.activation(q_hi[:], proj_bank[n % 2][:], ACT.Identity, bias=bias_q[own][:, u:u + 1]).then_inc(proj_hi_ready, 1)

        def exponentials(g, u):
            for j in range(UNIT):
                act.wait_ge(masked, UNIT * (C * g + u) + j + 1)
                nc.scalar.activation(probs[:, j, :], probs[:, j, :], ACT.Exp, bias=minus_max[:, j:j + 1], scale=-1.0,
                                     accum_out=row_sum[:, u % 2, j:j + 1]).then_inc(exped, 1)

        def transposed_high(g, u, h):
            act.wait_ge(pt_ready, 2 * (C * g + u) + h + 1)
            nc.scalar.copy(pt_hi[:, 4 * h:4 * h + 4, :], pt_bank[h][:].rearrange("p (j i) -> p j i", j=4)).then_inc(pt_hi_ready, 1)

        def split_queries(g, chunks):
            if chunks[0] == 0:
                act.wait_ge(query_in, 16 * (g - NG) + 16)
                if opens(g):
                    act.wait_ge(weight_lo, 6 * C)
                else:
                    act.wait_ge(projected, PROJ * g)
            for c in chunks:
                nc.scalar.copy(query_hi[:, c, :], query_raw[:, c, :]).then_inc(query_hi_ready, 1)

        def split_source(g, parity, chunks):
            if chunks[0] == 0:
                act.wait_ge(source_in, 16 * g + 32)
            for c in chunks:
                nc.scalar.copy(source_hi[1 - parity][:, c, :], source_raw[:, c, :]).then_inc(source_hi_ready, 1)

        def weights_ahead(g, own, after, u):
            if own == after:
                return
            if u == 0:
                act.wait_ge(projected, PROJ * g + VALUE_PLACE[GB - 1] + 1)
            if after == 1:
                weights_high(1, "v", AHEAD[u])
            elif 0 < u < 3:
                feed_forward.high(act, u - 1)

        def body(g, parity, before, own, after):
            if ends(g):
                transposed_high(g - 1, C - 1, 0)
                transposed_high(g - 1, C - 1, 1)
                feed_forward.high(act, 2)
                feed_forward.high(act, 3)
                return
            for b in range(2):
                value_high(g, parity, b)
                if not starts(g):
                    transposed_high(g - 1, C - 1, b)
                if opens(g):
                    weights_high(own, "q", range(2 * b, 2 * b + 2))
            if own == 1 and opens(g):
                split_queries(g, range(0, 2))
            value_high(g, parity, 2)
            if own == 1 and opens(g):
                split_queries(g, range(2, 4))
            key_high(g, own, 0)
            query_high(g, own, 0)
            value_high(g, parity, 3)
            exponentials(g, 0)
            weights_ahead(g, own, after, 0)
            for u in range(1, C):
                turning = u == C - 1 and not starts(g)
                if turning:
                    copy_turned(act, g - 1, 0)
                transposed_high(g, u - 1, 0)
                key_high(g, own, u)
                query_high(g, own, u)
                if turning:
                    copy_turned(act, g - 1, 1)
                transposed_high(g, u - 1, 1)
                if u == 1:
                    split_source(g, parity, range(0, 2))
                if u == 2:
                    split_source(g, parity, range(2, 4))
                if turning:
                    copy_turned(act, g - 1, 2)
                if u == C - 1 and own == 1 and after == 1:
                    split_queries(g + 1, range(C))
                exponentials(g, u)
                weights_ahead(g, own, after, u)
                if turning:
                    copy_turned(act, g - 1, 3)
            if own != after:
                act.wait_ge(projected, PROJ * NG * after)
                if after == 1:
                    weights_high(1, "k")

        over_passes(act, body)

    def inverse_spread(pool, g):
        pool_gate(pool, moments_ready, GB * g + GB, pool_scratch)
        nc.gpsimd.tensor_scalar(spread[:], moments[:, :, 1], EPS, None, ALU.add).then_inc(spread_ready, 1)
        pool.wait_ge(spread_ready, g + 1)
        nc.gpsimd.tensor_tensor(rstd[:], spread[:], half[:], ALU.pow).then_inc(rstd_ready, 1)

    def gain_and_shift(pool, g):
        for b in range(GB):
            pool.wait_ge(centred, GB * g + b + 1)
            nc.gpsimd.tensor_tensor(normed[:, b, :], normed[:, b, :], gain_row[:], ALU.mult).then_inc(gained, 1)
            pool.wait_ge(gained, GB * g + b + 1)
            nc.gpsimd.tensor_tensor(normed[:, b, :], normed[:, b, :], shift_row[:], ALU.add).then_inc(shifted, 1)

    @block.gpsimd
    def _(pool):
        nc.gpsimd.memset(half[:], -0.5).then_inc(zeroed, 1)
        nc.gpsimd.memset(pool_scratch[:], 0.0).then_inc(zeroed, 1)
        pool.wait_ge(zeroed, 6)

        def value_low(g, parity, b):
            pool_gate(pool, proj_split, PROJ * g + VALUE_PLACE[b] + 1, pool_scratch)
            nc.gpsimd.tensor_copy(v_part[parity][1][:, b, :], v_rest[:, b % 2, :]).then_inc(v_middle_ready, 1)
            pool.wait_ge(v_middle_ready, GB * g + b + 1)
            nc.gpsimd.tensor_tensor(v_part[parity][2][:, b, :], v_rest[:, b % 2, :], v_part[parity][1][:, b, :],
                                    ALU.subtract).then_inc(values_ready, 1)

        def split_queries(g, chunks):
            for c in chunks:
                pool.wait_ge(query_hi_ready, C * (g - NG) + c + 1)
                nc.gpsimd.tensor_tensor(query_lo[:, c, :], query_raw[:, c, :], query_hi[:, c, :].bitcast(F32),
                                        ALU.subtract).then_inc(query_ready, 1)

        def split_source(g, parity, chunks):
            for c in chunks:
                pool.wait_ge(source_hi_ready, C * g + C + c + 1)
                nc.gpsimd.tensor_tensor(source_lo[1 - parity][:, c, :], source_raw[:, c, :],
                                        source_hi[1 - parity][:, c, :].bitcast(F32), ALU.subtract).then_inc(source_ready, 1)

        def body(g, parity, before, own, after):
            if ends(g):
                return
            for b in range(GB):
                value_low(g, parity, b)
            if not starts(g):
                inverse_spread(pool, g - 1)
            split_source(g, parity, range(0, 2))
            if isinstance(g, int) and g % NG == 1:
                pool.wait_ge(norm_in, 2 * 16 * (g // NG + 1))
            if not starts(g):
                gain_and_shift(pool, g - 1)
            split_source(g, parity, range(2, 4))
            if opens(g):
                pool.wait_ge(bias_v_in, 16 * own + 16)
            pool.wait_ge(tokens_in, 16 * g + 16)
            for b in range(GB):
                nc.gpsimd.tensor_tensor(tokens[:, b, :], tokens[:, b, :], bias_v[:], ALU.add).then_inc(biased, 1)
            if own == 1 and after == 1:
                split_queries(g + 1, range(C))

        over_passes(pool, body)

    def sum_and_stats(dve, g, own, b):
        if b == 0:
            dve.wait_ge(attended_ready, C * g + C)
            if own == 1:
                wait(dve, tokens_out, 16 * (g - NG))
        dve.wait_ge(biased, GB * g + b + 1)
        wait(dve, turned_ready, GB * g)
        nc.vector.tensor_tensor(normed[:, b, :], attended[:, b, :], tokens[:, b, :], ALU.add).then_inc(summed, 1)
        dve.wait_ge(summed, GB * g + b + 1)
        nc.vector.bn_stats(stats[:, b, :], normed[:, b, :]).then_inc(stats_ready, 1)
        gate(dve, stats_ready, GB * g + b + 1, dve_scratch[:, 2 + b:3 + b])
        nc.vector.bn_aggr(moments[:, b, :], stats[:, b, :]).then_inc(moments_ready, 1)

    def centre(dve, g, graphs):
        if graphs[0] == 0:
            dve.wait_ge(rstd_ready, g + 1)
        for b in graphs:
            nc.vector.tensor_scalar(normed[:, b, :], normed[:, b, :], moments[:, b, 0:1], rstd[:, b:b + 1],
                                    ALU.subtract, ALU.mult).then_inc(centred, 1)

    @block.vector
    def _(dve):
        nc.vector.memset(k_hi[HD:P, 0, :].bitcast(F32), 0.0).then_inc(zeroed, 1)
        nc.vector.memset(k_hi[0:HD, 1, :].bitcast(F32), 0.0).then_inc(zeroed, 1)
        nc.vector.memset(k_lo[HD:P, 0, :].bitcast(F32), 0.0).then_inc(zeroed, 1)
        nc.vector.memset(k_lo[0:HD, 1, :].bitcast(F32), 0.0).then_inc(zeroed, 1)

        def weights_low(n, w, chunks=range(C)):
            for c in chunks:
                dve.wait_ge(weight_hi, C * (3 * n + "vkq".index(w)) + c + 1)
                nc.vector.tensor_tensor(wl[w][:, c, :], weight_raw[w][:, c, :], wh[w][:, c, :].bitcast(F32),
                                        ALU.subtract).then_inc(weight_lo, 1)

        for c in range(C):
            dve.wait_ge(source_hi_ready, c + 1)
            nc.vector.tensor_tensor(source_lo[0][:, c, :], source_raw[:, c, :], source_hi[0][:, c, :].bitcast(F32),
                                    ALU.subtract).then_inc(source_ready, 1)
        for w in "vk":
            weights_low(0, w)
        dve.wait_ge(constants_in, 5 * 16)
        dve.wait_ge(zeroed, 6)

        def value_rest(g, parity, b):
            n = VALUE_PLACE[b]
            dve.wait_ge(proj_hi_ready, PROJ * g + n + 1)
            wait(dve, values_ready, GB * g + b - 1)
            nc.vector.tensor_tensor(v_rest[:, b % 2, :], proj_bank[n % 2][:], v_part[parity][0][:, b, :],
                                    ALU.subtract).then_inc(proj_split, 1)

        def key_low(g, own, u):
            n = KEY_PLACE[u]
            dve.wait_ge(key_half_ready, C * g + u + 1)
            nc.vector.scalar_tensor_tensor(k_lo[0:HD, 0, :], proj_bank[n % 2][0:HD, :], bias_k[own][0:HD, u:u + 1],
                                           k_hi[0:HD, 0, :].bitcast(F32), ALU.add, ALU.subtract)
            dve.wait_ge(proj_hi_ready, PROJ * g + n + 1)
            nc.vector.scalar_tensor_tensor(k_lo[HD:P, 1, :], proj_bank[n % 2][HD:P, :], bias_k[own][HD:P, u:u + 1],
                                           k_hi[HD:P, 1, :].bitcast(F32), ALU.add, ALU.subtract).then_inc(proj_split, 1)

        def query_low(g, own, u):
            n = QUERY_PLACE[u]
            dve.wait_ge(proj_hi_ready, PROJ * g + n + 1)
            nc.vector.scalar_tensor_tensor(q_lo[:], proj_bank[n % 2][:], bias_q[own][:, u:u + 1], q_hi[:].bitcast(F32),
                                           ALU.add, ALU.subtract).then_inc(proj_split, 1)

        def mask_and_maximum(g, u):
            if u == 0:
                dve.wait_ge(mask_ready, g + 1)
            for h in range(2):
                gate(dve, scored, 2 * (C * g + u) + h + 1, dve_scratch[:, h:h + 1])
                for j in range(4):
                    nc.vector.tensor_tensor_reduce(
                        out=probs[:, 4 * h + j, :], in0=score_bank[h][:, j * P:(j + 1) * P],
                        in1=mask[:, 2 * h + j // 2, :], scale=-SCALE, scalar=LARGEST, op0=ALU.add, op1=ALU.min,
                        accum_out=minus_max[:, 4 * h + j:4 * h + j + 1]).then_inc(masked, 1)

        def transposed_low(g, u, h):
            dve.wait_ge(pt_hi_ready, 2 * (C * g + u) + h + 1)
            nc.vector.tensor_tensor(pt_lo[:, 4 * h:4 * h + 4, :], pt_bank[h][:].rearrange("p (j i) -> p j i", j=4),
                                    pt_hi[:, 4 * h:4 * h + 4, :], ALU.subtract).then_inc(pt_split, 1)

        def divide(g, u):
            dve.wait_ge(exped, UNIT * (C * g + u + 1))
            nc.vector.reciprocal(row_inverse[:, u % 2, :], row_sum[:, u % 2, :]).then_inc(inverted, 1)
            dve.wait_ge(inverted, C * g + u + 1)
            dve.wait_ge(weighed, C * g + u + 1)
            nc.vector.tensor_tensor(
                attended[:, :, u * P:(u + 1) * P].rearrange("p b (h d) -> p b h d", h=2),
                out_bank[:].rearrange("p (b h d) -> p b h d", b=GB, h=2),
                row_inverse[:, u % 2, :].rearrange("p (b h o) -> p b h o", b=GB, o=1).to_broadcast([P, GB, 2, HD]),
                ALU.mult).then_inc(attended_ready, 1)

        def weights_ahead(own, after, u):
            if own == after:
                return
            if after == 1:
                weights_low(1, "v", AHEAD[u])
            elif 0 < u < 3:
                feed_forward.low(dve, u - 1)

        def first_queries(g, own, chunks):
            if not (own == 1 and opens(g)):
                return
            for c in chunks:
                dve.wait_ge(query_hi_ready, c + 1)
                nc.vector.tensor_tensor(query_lo[:, c, :], query_raw[:, c, :], query_hi[:, c, :].bitcast(F32),
                                        ALU.subtract).then_inc(query_ready, 1)

        def body(g, parity, before, own, after):
            if ends(g):
                transposed_low(g - 1, C - 1, 0)
                transposed_low(g - 1, C - 1, 1)
                feed_forward.low(dve, 2)
                divide(g - 1, C - 1)
                feed_forward.low(dve, 3)
                return
            dve.wait_ge(adj_in, 16 * g + 16)
            wait(dve, masked, UNIT * C * g)
            nc.vector.tensor_scalar(mask[:], adj[:], 0.0, MASKED, ALU.is_le, ALU.mult).then_inc(mask_ready, 1)
            for b in range(2):
                value_rest(g, parity, b)
                if not starts(g):
                    transposed_low(g - 1, C - 1, b)
                if opens(g):
                    weights_low(own, "q", range(2 * b, 2 * b + 2))
            first_queries(g, own, range(0, 2))
            value_rest(g, parity, 2)
            first_queries(g, own, range(2, 4))
            if not starts(g):
                divide(g - 1, C - 1)
                sum_and_stats(dve, g - 1, before, 0)
            key_low(g, own, 0)
            if not starts(g):
                sum_and_stats(dve, g - 1, before, 1)
            query_low(g, own, 0)
            if not starts(g):
                sum_and_stats(dve, g - 1, before, 2)
            value_rest(g, parity, 3)
            mask_and_maximum(g, 0)
            weights_ahead(own, after, 0)
            if not starts(g):
                sum_and_stats(dve, g - 1, before, 3)
            for u in range(1, C):
                transposed_low(g, u - 1, 0)
                key_low(g, own, u)
                query_low(g, own, u)
                transposed_low(g, u - 1, 1)
                if u == 1 and not starts(g):
                    centre(dve, g - 1, range(0, 2))
                mask_and_maximum(g, u)
                divide(g, u - 1)
                weights_ahead(own, after, u)
                if u == 1 and not starts(g):
                    centre(dve, g - 1, range(2, GB))
            if own != after and after == 1:
                weights_low(1, "k")

        over_passes(dve, body)

    def turn(pe, g, b):
        pe.wait_ge(shifted, GB * g + b + 1)
        wait(pe, turned_copied, GB * g + b)
        for c in range(C):
            last = nc.tensor.transpose(turn_bank[:, c * P:(c + 1) * P], normed[:, b, c * P:(c + 1) * P], identity[:])
        last.then_inc(turned_ready, 1)

    @block.tensor
    def _(pe):
        def parts(a, b):
            return ((a[0], b[0]), (a[0], b[1]), (a[1], b[0]))

        def project(g, n, products, chunks=range(C)):
            if chunks[0] == 0:
                wait(pe, proj_split, PROJ * g + n - 1)
            for c in chunks:
                for i, (stationary, moving) in enumerate(products(c)):
                    last = nc.tensor.matmul(proj_bank[n % 2][:], stationary, moving, start=(c == 0 and i == 0),
                                            stop=(c == C - 1 and i == 2))
            if chunks[-1] == C - 1:
                last.then_inc(projected, 1)

        def values(g, parity, own, b):
            if b == 0:
                pe.wait_ge(source_ready, C * g + C)
            x = [s[parity] for s in (source_hi, source_lo)]
            for c in range(C):
                if opens(g) and b == 0:
                    pe.wait_ge(weight_lo, 3 * C * own + c + 1)
                project(g, VALUE_PLACE[b], lambda c: parts([s[:, c, b * P:(b + 1) * P] for s in x],
                                                           [w[:, c, :] for w in (wh["v"], wl["v"])]), range(c, c + 1))

        def keys(g, parity, own, u, chunks=range(C)):
            if opens(g) and u == 0:
                pe.wait_ge(weight_lo, 3 * C * own + 2 * C)
            x = [s[parity] for s in (source_hi, source_lo)]
            project(g, KEY_PLACE[u], lambda c: parts([w[:, c, u * P:(u + 1) * P] for w in (wh["k"], wl["k"])],
                                                   [s[:, c, :] for s in x]), chunks)

        def queries(g, parity, own, u):
            if u == 0:
                if own == 1:
                    pe.wait_ge(query_ready, C * (g - NG) + C)
                if opens(g):
                    pe.wait_ge(weight_lo, 3 * C * own + 3 * C)
            x = (query_hi, query_lo) if own == 1 else [s[parity] for s in (source_hi, source_lo)]
            project(g, QUERY_PLACE[u], lambda c: parts([w[:, c, u * P:(u + 1) * P] for w in (wh["q"], wl["q"])],
                                                       [s[:, c, :] for s in x]))

        def scores(g, u):
            if starts(g) and u == 0:
                pe.wait_ge(zeroed, 6)
                pe.wait_ge(constants_in, 5 * 16)
            pe.wait_ge(proj_split, PROJ * g + QUERY_PLACE[u] + 1)
            for h in range(2):
                for i in range(2):
                    b = 2 * h + i
                    products = parts([q[:, b * P:(b + 1) * P] for q in (q_hi, q_lo)],
                                     [k[:, :, b * P:(b + 1) * P] for k in (k_hi, k_lo)])
                    for n, (q, k) in enumerate(products):
                        last = nc.tensor.matmul(
                            score_bank[h][:, 2 * i * P:2 * (i + 1) * P].rearrange("p (s j) -> p s j", s=2), q, k,
                            start=(n == 0), stop=(n == 2))
                last.then_inc(scored, 1)

        def transposes(g, u, h):
            pe.wait_ge(exped, UNIT * (C * g + u) + 4 * (h + 1))
            for j in range(4):
                last = nc.tensor.transpose(pt_bank[h][:, j * P:(j + 1) * P], probs[:, 4 * h + j, :], identity[:])
            last.then_inc(pt_ready, 1)

        def weigh(g, parity, u, h):
            if u == 0:
                pe.wait_ge(values_ready, GB * g + 2 * h + 2)
            if h == 0:
                wait(pe, attended_ready, C * g + u)
            pe.wait_ge(pt_split, 2 * (C * g + u) + h + 1)
            for j in range(4):
                b, column = 2 * h + j // 2, u * P + (j % 2) * HD
                v = [part[:, b, column:column + HD] for part in v_part[parity]]
                hi, lo = pt_hi[:, 4 * h + j, :], pt_lo[:, 4 * h + j, :]
                out = out_bank[:, (4 * h + j) * HD:(4 * h + j + 1) * HD]
                products = ((hi, v[0]), (hi, v[1]), (hi, v[2]), (lo, v[0]), (lo, v[1]))
                for n, (p, value) in enumerate(products):
                    last = nc.tensor.matmul(out, p, value, start=(n == 0), stop=(n == len(products) - 1))
            if h == 1:
                last.then_inc(weighed, 1)

        def body(g, parity, before, own, after):
            if ends(g):
                transposes(g - 1, C - 1, 0)
                transposes(g - 1, C - 1, 1)
                weigh(g - 1, 1 - parity, C - 1, 0)
                weigh(g - 1, 1 - parity, C - 1, 1)
                return
            values(g, parity, own, 0)
            if not starts(g):
                transposes(g - 1, C - 1, 0)
            values(g, parity, own, 1)
            if not starts(g):
                transposes(g - 1, C - 1, 1)
            values(g, parity, own, 2)
            if not starts(g):
                weigh(g - 1, 1 - parity, C - 1, 0)
                weigh(g - 1, 1 - parity, C - 1, 1)
            keys(g, parity, own, 0)
            queries(g, parity, own, 0)
            values(g, parity, own, 3)
            scores(g, 0)
            for u in range(1, C):
                turning = u == C - 1 and not starts(g)
                keys(g, parity, own, u, range(1 if u > 1 else 0, C))
                transposes(g, u - 1, 0)
                queries(g, parity, own, u)
                if turning:
                    turn(pe, g - 1, 1)
                transposes(g, u - 1, 1)
                weigh(g, parity, u - 1, 0)
                if turning:
                    turn(pe, g - 1, 2)
                if u < C - 1:
                    keys(g, parity, own, u + 1, range(1))
                scores(g, u)
                weigh(g, parity, u - 1, 1)
                if turning:
                    turn(pe, g - 1, 3)
                if u == C - 2 and not starts(g):
                    turn(pe, g - 1, 0)

        over_passes(pe, body)

    last = last_group - 1
    return {
        "turn": lambda pe, b: turn(pe, last, b),
        "copy_turned": lambda act, b: copy_turned(act, last, b),
        "store": store_last,
        "store_tokens": store_last_tokens,
        "sum_and_stats": lambda dve, b: sum_and_stats(dve, last, 1, b),
        "centre": lambda dve: centre(dve, last, range(GB)),
        "inverse_spread": lambda pool: inverse_spread(pool, last),
        "gain_and_shift": lambda pool: gain_and_shift(pool, last),
        "banks_free": ((proj_split, PROJ * last_group), (masked, UNIT * C * last_group), (pt_split, 2 * C * last_group)),
        "residual_biased": (biased, GB * last_group),
    }


def feed_forward_pass(nc, ctx, m, block, weights, attention, source, nodes, x, b1, b2, gain, shift, out):
    def starts(group):
        return isinstance(group, int) and group == 0

    def ends(group):
        return isinstance(group, int) and group == NG

    def whole(group):
        return not (isinstance(group, int) and group >= NG - 1)

    def sem(n):
        return ctx.enter_context(nc.semaphore(f"ffn_{n}"))

    source_raw, source_hi, source_lo = m.source_raw, m.source_hi, m.source_lo
    bias_2, gain_row, shift_row, half = m.bias_row, m.gain_row, m.shift_row, m.half
    hidden, hidden_hi, hidden_lo = weights.hidden, weights.hidden_hi, weights.hidden_lo
    tokens = m.normed
    x_tile = m.turned[:].rearrange("p i c t -> p i (c t)")
    bias_1 = m.feed_forward["bias_1"]
    pool_scratch = m.pool_scratch
    dve_scratch, stats, moments, spread, rstd = (m.feed_forward[n] for n in NORM_TILES)

    up_bank = m.proj_bank
    down_bank = m.score_bank + m.pt_bank

    bias_1_in, tokens_in = sem("bias_1_in"), sem("tokens_in")
    source_in, source_hi_ready, source_ready = m.source_in, m.source_hi_ready, m.source_ready
    x_in = [sem("x_in0"), sem("x_in1")]
    before = 2 * NG
    raised, activated, hidden_hi_ready, hidden_ready = sem("raised"), sem("activated"), sem("hidden_hi_ready"), sem("hidden_ready")
    lowered, biased, summed = sem("lowered"), sem("biased"), sem("summed")
    stats_ready, moments_ready = sem("stats_ready"), sem("moments_ready")
    spread_ready, rstd_ready, centred = sem("spread_ready"), sem("rstd_ready"), sem("centred")
    gained, shifted, topped = sem("gained"), sem("shifted"), sem("topped")
    odd_step = sem("odd_step")
    stored, last_stored = sem("stored"), sem("last_stored")

    source_view = source.rearrange("(c p) t -> p c t", p=P)
    nodes_view = nodes.rearrange("(b p) d -> p b d", p=P)
    x_view = x.rearrange("(b p) d -> p b d", p=P)
    out_view = out.rearrange("(b p) d -> p b d", p=P)
    AHEAD = 4
    TURNS = 8
    SPLIT = 8

    @block.sync
    def _(sp):
        sp.dma_start(bias_1[:], b1).then_inc(bias_1_in, 16)
        sp.wait_ge(*attention["residual_biased"])
        sp.dma_start(bias_2[:], row(b2)).then_inc(m.bias_row_in, 16)

        def load_source(g):
            wait(sp, source_ready, C * (before + g))
            for s in m.turned_out:
                sp.wait_ge(s, 32 * (NG + g + 1))
            sp.dma_start(source_raw[:], source_view[:, :, bass.ds(g * GT, GT)]).then_inc(source_in, 16)

        load_source(1)
        for n in range(AHEAD, len(weights.pieces)):
            weights.load(sp, n)
        for b in range(GB):
            attention["store"](sp, b)
        attention["store_tokens"](sp)
        for tile, data in ((gain_row[:], row(gain)), (shift_row[:], row(shift))):
            sp.dma_start(tile, data).then_inc(m.norm_in, 16)

        def body(g, parity):
            if whole(g) and not starts(g):
                load_source(g + 1)
            if not starts(g):
                for b in range(GB):
                    n = GB * (g - 1) + b
                    if b < 2 and isinstance(g, int) and g == 1:
                        sp.wait_ge(m.turned_out[b], 32 * before)
                    if b >= 2:
                        if ends(g) and b % 2 == 1:
                            sp.wait_ge(odd_step, 3)
                        else:
                            sp.wait_ge(topped, GB * (g - 1) + (1 if ends(g) else b - 1))
                    sp.dma_start(x_tile[:, b % 2, :], x_view[:, (g - 1) * GB + b, :] if isinstance(g, int)
                                 else x_view[:, bass.ds((g - 1) * GB + b, 1), :].rearrange("p b d -> p (b d)")).then_inc(x_in[b % 2], 16)
                if ends(g):
                    for b in range(GB):
                        sp.wait_ge(centred, 2 * GB * (g - 1) + GB + b + 1)
                        sp.dma_start(out_view[:, (g - 1) * GB + b, :], tokens[:, b, :]).then_inc(last_stored, 16)
                    return
                wait(sp, centred, 2 * GB * g)
                sp.dma_start(out_view[:, bass.ds((g - 1) * GB, GB), :], tokens[:]).then_inc(stored, 16)
            if not ends(g):
                wait(sp, stored, 16 * g)
                sp.dma_start(tokens[:], nodes_view[:, bass.ds(g * GB, GB), :]).then_inc(tokens_in, 16)

        over_groups(sp, body)
        body(NG, 0)
        sp.wait_ge(stored, 16 * (NG - 1))
        sp.wait_ge(last_stored, 16 * GB)

    @block.scalar
    def _(act):
        act.wait_ge(bias_1_in, 16)

        def hidden_high(g, c):
            act.wait_ge(activated, FC * g + c + 1)
            nc.scalar.copy(hidden_hi[:, c % 2, :], hidden[:, c % 2, :]).then_inc(hidden_hi_ready, 1)

        def body(g, parity):
            for c in range(FC):
                act.wait_ge(raised, FC * g + c + 1)
                wait(act, hidden_ready, FC * g + c - 1)
                nc.scalar.activation(hidden[:, c % 2, :], up_bank[c % 2][:], ACT.Gelu,
                                     bias=bias_1[:, c:c + 1]).then_inc(activated, 1)
                hidden_high(g, c)
                if starts(g) and AHEAD + c < len(weights.pieces):
                    weights.high(act, AHEAD + c)
                if SPLIT <= c < SPLIT + C and whole(g):
                    if c == SPLIT:
                        act.wait_ge(source_in, 16 * (before + g) + 32)
                    nc.scalar.copy(source_hi[1 - parity][:, c - SPLIT, :], source_raw[:, c - SPLIT, :]).then_inc(source_hi_ready, 1)
                if starts(g) and TURNS <= c < TURNS + GB:
                    attention["copy_turned"](act, c - TURNS)

        over_groups(act, body)

    @block.gpsimd
    def _(pool):
        attention["inverse_spread"](pool)
        attention["gain_and_shift"](pool)

        def finish():
            g = NG - 1
            done = 2 * g
            for pair in range(2):
                graphs = slice(2 * pair, 2 * pair + 2)
                pool.wait_ge(moments_ready, 2 * GB * g + 2 * pair + 2)
                nc.gpsimd.tensor_scalar(spread[:, graphs], moments[:, graphs, 1], EPS, None, ALU.add).then_inc(spread_ready, 1)
                pool.wait_ge(spread_ready, done + pair + 1)
                nc.gpsimd.tensor_tensor(rstd[:, graphs], spread[:, graphs], half[:, graphs], ALU.pow).then_inc(rstd_ready, 1)
            for n, b in enumerate((0, 2)):
                step = GB * g + n + 1
                pool.wait_ge(centred, 2 * GB * g + b + 1)
                nc.gpsimd.tensor_tensor(tokens[:, b, :], tokens[:, b, :], gain_row[:], ALU.mult).then_inc(gained, 1)
                pool.wait_ge(gained, step)
                nc.gpsimd.tensor_tensor(tokens[:, b, :], tokens[:, b, :], shift_row[:], ALU.add).then_inc(shifted, 1)
                pool.wait_ge(shifted, step)
                pool.wait_ge(x_in[0], 16 * (2 * g + n + 1))
                nc.gpsimd.tensor_tensor(tokens[:, b, :], tokens[:, b, :], x_tile[:, 0, :], ALU.add).then_inc(topped, 1)
            pool.wait_ge(moments_ready, 2 * GB * NG)
            pool.wait_ge(centred, 2 * GB * g + GB)
            nc.gpsimd.tensor_scalar(spread[:], moments[:, :, 1], EPS, None, ALU.add).then_inc(spread_ready, 1)
            pool.wait_ge(spread_ready, done + 3)
            nc.gpsimd.tensor_tensor(rstd[:], spread[:], half[:], ALU.pow).then_inc(rstd_ready, 1)

        def inverse_spread(g, norm):
            n = 2 * g + norm
            pool_gate(pool, moments_ready, GB * (n + 1), pool_scratch)
            nc.gpsimd.tensor_scalar(spread[:], moments[:, :, 1], EPS, None, ALU.add).then_inc(spread_ready, 1)
            pool.wait_ge(spread_ready, n + 1)
            nc.gpsimd.tensor_tensor(rstd[:], spread[:], half[:], ALU.pow).then_inc(rstd_ready, 1)

        def body(g, parity):
            if not starts(g):
                inverse_spread(g - 1, 0)
                if isinstance(g, int) and g == 1:
                    pool.wait_ge(m.norm_in, 3 * 2 * 16)
                for b in range(GB):
                    n = GB * (g - 1) + b + 1
                    pool.wait_ge(centred, 2 * GB * (g - 1) + b + 1)
                    nc.gpsimd.tensor_tensor(tokens[:, b, :], tokens[:, b, :], gain_row[:], ALU.mult).then_inc(gained, 1)
                    pool.wait_ge(gained, n)
                    nc.gpsimd.tensor_tensor(tokens[:, b, :], tokens[:, b, :], shift_row[:], ALU.add).then_inc(shifted, 1)
                    pool.wait_ge(shifted, n)
                    pool.wait_ge(x_in[b % 2], 16 * (2 * (g - 1) + b // 2 + 1))
                    nc.gpsimd.tensor_tensor(tokens[:, b, :], tokens[:, b, :], x_tile[:, b % 2, :], ALU.add).then_inc(topped, 1)
                inverse_spread(g - 1, 1)
            if whole(g):
                for c in range(C):
                    pool.wait_ge(source_hi_ready, C * (before + g) + C + c + 1)
                    nc.gpsimd.tensor_tensor(source_lo[1 - parity][:, c, :], source_raw[:, c, :],
                                            source_hi[1 - parity][:, c, :].bitcast(F32), ALU.subtract).then_inc(source_ready, 1)
            if not ends(g):
                if starts(g):
                    pool.wait_ge(m.bias_row_in, 3 * 16)
                pool.wait_ge(tokens_in, 16 * g + 16)
                for b in range(GB):
                    nc.gpsimd.tensor_tensor(tokens[:, b, :], tokens[:, b, :], bias_2[:], ALU.add).then_inc(biased, 1)

        over_groups(pool, body)
        finish()

    @block.vector
    def _(dve):
        def moments_of(g, norm, b):
            n = 2 * GB * g + GB * norm + b + 1
            nc.vector.bn_stats(stats[:, b, :], tokens[:, b, :]).then_inc(stats_ready, 1)
            gate(dve, stats_ready, n, dve_scratch[:, b:b + 1])
            nc.vector.bn_aggr(moments[:, b, :], stats[:, b, :]).then_inc(moments_ready, 1)

        def centre(g, norm):
            dve.wait_ge(rstd_ready, 2 * g + norm + 1)
            for b in range(GB):
                nc.vector.tensor_scalar(tokens[:, b, :], tokens[:, b, :], moments[:, b, 0:1], rstd[:, b:b + 1],
                                        ALU.subtract, ALU.mult).then_inc(centred, 1)

        def finish():
            g = NG - 1

            def second_moments(n, b):
                dve.wait_ge(centred, 2 * GB * g + GB)
                if b % 2 == 0:
                    dve.wait_ge(topped, GB * g + b // 2 + 1)
                else:
                    dve.wait_ge(odd_step, 3 * (b // 2) + 3)
                nc.vector.bn_stats(stats[:, b, :], tokens[:, b, :]).then_inc(stats_ready, 1)
                dve.wait_ge(stats_ready, 2 * GB * g + GB + n + 1)
                nc.vector.bn_aggr(moments[:, b, :], stats[:, b, :]).then_inc(moments_ready, 1)

            for b in range(GB):
                dve.wait_ge(lowered, GB * g + b + 1)
                dve.wait_ge(biased, GB * g + b + 1)
                nc.vector.tensor_tensor(tokens[:, b, :], down_bank[b][:], tokens[:, b, :], ALU.add).then_inc(summed, 1)
                dve.wait_ge(summed, GB * g + b + 1)
                moments_of(g, 0, b)
            for b in range(GB):
                dve.wait_ge(rstd_ready, 2 * g + b // 2 + 1)
                nc.vector.tensor_scalar(tokens[:, b, :], tokens[:, b, :], moments[:, b, 0:1], rstd[:, b:b + 1],
                                        ALU.subtract, ALU.mult).then_inc(centred, 1)
            for n, b in enumerate((1, 3)):
                dve.wait_ge(centred, 2 * GB * g + b + 1)
                nc.vector.tensor_tensor(tokens[:, b, :], tokens[:, b, :], gain_row[:], ALU.mult).then_inc(odd_step, 1)
                dve.wait_ge(odd_step, 3 * n + 1)
                nc.vector.tensor_tensor(tokens[:, b, :], tokens[:, b, :], shift_row[:], ALU.add).then_inc(odd_step, 1)
                dve.wait_ge(odd_step, 3 * n + 2)
                dve.wait_ge(x_in[1], 16 * (2 * g + n + 1))
                if b == 3:
                    second_moments(0, 1)
                    second_moments(1, 0)
                nc.vector.tensor_tensor(tokens[:, b, :], tokens[:, b, :], x_tile[:, 1, :], ALU.add).then_inc(odd_step, 1)
            second_moments(2, 3)
            second_moments(3, 2)
            dve.wait_ge(rstd_ready, 2 * g + 3)
            for b in range(GB):
                nc.vector.tensor_scalar(tokens[:, b, :], tokens[:, b, :], moments[:, b, 0:1], rstd[:, b:b + 1],
                                        ALU.subtract, ALU.mult).then_inc(centred, 1)

        def body(g, parity):
            for c in range(FC):
                if not ends(g):
                    dve.wait_ge(hidden_hi_ready, FC * g + c + 1)
                    nc.vector.tensor_tensor(hidden_lo[:, c % 2, :], hidden[:, c % 2, :], hidden_hi[:, c % 2, :].bitcast(F32),
                                            ALU.subtract).then_inc(hidden_ready, 1)
                if starts(g):
                    if AHEAD + c < len(weights.pieces):
                        weights.low(dve, AHEAD + c)
                    if c < GB:
                        attention["sum_and_stats"](dve, c)
                    if c == GB:
                        attention["centre"](dve)
                    continue
                if c == 0:
                    for b in range(GB):
                        dve.wait_ge(lowered, GB * (g - 1) + b + 1)
                        dve.wait_ge(biased, GB * (g - 1) + b + 1)
                        nc.vector.tensor_tensor(tokens[:, b, :], down_bank[b][:], tokens[:, b, :], ALU.add).then_inc(summed, 1)
                if 2 <= c < 2 + GB:
                    b = c - 2
                    dve.wait_ge(summed, GB * (g - 1) + b + 1)
                    moments_of(g - 1, 0, b)
                if c == 6:
                    centre(g - 1, 0)
                if c == 10:
                    for b in range(GB):
                        dve.wait_ge(topped, GB * (g - 1) + b + 1)
                        moments_of(g - 1, 1, b)
                if c == 12:
                    centre(g - 1, 1)

        over_groups(dve, body)
        finish()

    @block.tensor
    def _(pe):
        for semaphore, value in attention["banks_free"]:
            pe.wait_ge(semaphore, value)

        def parts(a, b):
            return ((a[0], b[0]), (a[0], b[1]), (a[1], b[0]))

        def up(g, parity, c):
            if c == 0:
                pe.wait_ge(source_ready, C * (before + g) + C)
            if starts(g) and c % 4 == 0:
                pe.wait_ge(weights.ready, c + 2)
            wait(pe, activated, FC * g + c - 1)
            products = [p for k in range(C)
                        for p in parts([w[:, k, (c % 4) * P:(c % 4 + 1) * P] for w in weights.w1[c // 4]],
                                       [s[parity][:, k, :] for s in (source_hi, source_lo)])]
            for i, (w, s) in enumerate(products):
                last = nc.tensor.matmul(up_bank[c % 2][:], w, s, start=(i == 0), stop=(i == len(products) - 1))
            last.then_inc(raised, 1)

        def down(g, c):
            if starts(g) and c % 4 == 0:
                pe.wait_ge(weights.ready, c + 4)
            pe.wait_ge(hidden_ready, FC * g + c + 1)
            if c == 0:
                wait(pe, summed, GB * g)
            for b in range(GB):
                products = parts([h[:, c % 2, b * P:(b + 1) * P] for h in (hidden_hi, hidden_lo)],
                                 [w[:, c % 4, :] for w in weights.w2[c // 4]])
                for i, (h, w) in enumerate(products):
                    last = nc.tensor.matmul(down_bank[b][:], h, w, start=(c == 0 and i == 0), stop=(c == FC - 1 and i == 2))
                if c == FC - 1:
                    last.then_inc(lowered, 1)

        def body(g, parity):
            for c in range(FC):
                if not ends(g):
                    up(g, parity, c)
                if starts(g) and TURNS <= c < TURNS + GB:
                    attention["turn"](pe, c - TURNS)
                if c > 0 and not ends(g):
                    down(g, c - 1)
                if c == 0 and not starts(g):
                    down(g - 1, FC - 1)

        over_groups(pe, body)
        body(NG, 0)


def build(nc, xt, x, adj_t, adj, ident, n2e, e2n, ffn, scratch, out):
    with ExitStack() as ctx:
        m = Shared(nc, ctx)
        weights = FeedForwardWeights(nc, ctx, m, ffn["w1"], ffn["w2"])
        block = ctx.enter_context(nc.Block())
        last_norm = attention_passes(nc, ctx, m, block, (
            {"source": xt, "adjacency": adj_t, "out_features": scratch["edges_t"], **n2e},
            {"source": scratch["edges_t"], "query_source": xt, "adjacency": adj, "out_features": scratch["nodes_t"],
             "out_tokens": scratch["nodes"], **e2n}), weights, scratch["nodes_t"], x, ident)
        feed_forward_pass(nc, ctx, m, block, weights, last_norm, scratch["nodes_t"], scratch["nodes"], x,
                          ffn["b1"], ffn["b2"], ffn["gain"], ffn["shift"], out)


def kernel(**inputs):
    import numpy as np
    import concourse.bacc as bacc
    from concourse.bass_utils import run_bass_kernel_spmd

    def weights_t(name):
        return np.ascontiguousarray(np.asarray(inputs["L0_gnn_" + name]).T)

    def vector(name):
        return np.ascontiguousarray(inputs["L0_gnn_" + name])

    def columns(name):
        return np.ascontiguousarray(vector(name).reshape(-1, P).T)

    x = np.ascontiguousarray(inputs["x"]).reshape(T, D)
    adj = np.asarray(inputs["adj"])
    arrays = {
        "x": x,
        "x_t": np.ascontiguousarray(x.T),
        "adj_nodes": np.ascontiguousarray(adj.transpose(1, 0, 2)),
        "adj_edges": np.ascontiguousarray(adj.transpose(2, 0, 1)),
        "identity": np.eye(P, dtype=np.float32),
    }
    for side, norm in (("n2e", "norm1"), ("e2n", "norm2")):
        for p in "qkv":
            arrays[f"{side}_{p}_w"] = weights_t(f"{side}_{p}_w")
        for p in "qk":
            arrays[f"{side}_{p}_b"] = columns(f"{side}_{p}_b")
        arrays[f"{side}_v_b"] = vector(f"{side}_v_b")
        for p in "gb":
            arrays[f"{side}_norm_{p}"] = vector(f"{norm}_{p}")
    arrays |= {"w1": weights_t("ffn_w1"), "b1": columns("ffn_b1"), "w2": weights_t("ffn_w2"), "b2": vector("ffn_b2"),
               "norm_g": vector("norm3_g"), "norm_b": vector("norm3_b")}

    nc = bacc.Bacc("TRN2", target_bir_lowering=False, num_devices=1)
    a = {}
    for name, array in arrays.items():
        a[name] = nc.dram_tensor(f"in_{name}", array.shape, mybir.dt.from_np(array.dtype), kind="ExternalInput").ap()
    out = nc.dram_tensor("out", (T, D), F32, kind="ExternalOutput").ap()
    scratch = {"edges_t": nc.dram_tensor("edges_t", (D, T), F32).ap(),
               "nodes_t": nc.dram_tensor("nodes_t", (D, T), F32).ap(),
               "nodes": nc.dram_tensor("nodes", (T, D), F32).ap()}

    def side(s):
        names = {"wq": "q_w", "wk": "k_w", "wv": "v_w", "bq": "q_b", "bk": "k_b", "bv": "v_b", "gain": "norm_g", "shift": "norm_b"}
        return {role: a[f"{s}_{n}"] for role, n in names.items()}

    build(nc, a["x_t"], a["x"], a["adj_edges"], a["adj_nodes"], a["identity"], side("n2e"), side("e2n"),
          {"w1": a["w1"], "b1": a["b1"], "w2": a["w2"], "b2": a["b2"], "gain": a["norm_g"], "shift": a["norm_b"]}, scratch, out)
    result = run_bass_kernel_spmd(nc, [{f"in_{n}": v for n, v in arrays.items()}], core_ids=[0])
    return result.results[0]["out"].reshape(B, P, D)
```
